# Optimizing a Trainium2 kernel written in Bass

```python
import numpy as np
import jax
import jax.numpy as jnp

def _softmax(x, axis=-1):
    return jax.nn.softmax(x, axis=axis)
def _gelu(x):
    return jax.nn.gelu(x, approximate=True)
def _silu(x):
    return jax.nn.silu(x)
def _sigmoid(x):
    return jax.nn.sigmoid(x)
def _layernorm(x, axis=-1, eps=1e-5):
    m = jnp.mean(x, axis=axis, keepdims=True)
    v = jnp.var(x, axis=axis, keepdims=True)
    return (x - m) / jnp.sqrt(v + eps)
def _scatter_add(tgt, idx, src, axis=0):
    return tgt.at[idx].add(src)
def _segment_sum(src, seg, n):
    return jax.ops.segment_sum(src, seg, n)

kernel_name = 'mk_adj_preln_d2_adj_512_ff51d0'

def setup_inputs(seed: int = 0):
    np.random.seed(seed)
    _w = jnp.asarray
    def _rec_inputs():
        import jax
        import jax.numpy as jnp
        _gk = jax.random.key(seed)
        x = -0.000125 + 0.9999 * jax.random.normal(jax.random.fold_in(_gk, 1), (16, 1024, 512), jnp.float32)
        _a = jax.random.bernoulli(jax.random.fold_in(_gk, 2), 0.03125, (1024, 1024))
        _af = _a.astype(jnp.float32)
        adj = _af
        return x, adj
    x, adj = _rec_inputs()
    def _L0_gnn_setup():
        import jax, jax.numpy as jnp
        import numpy as np
        ALPHA = 0.2
        key = jax.random.key(seed)
        k0, k1, k2, k3 = jax.random.split(key, 4)
        B, N, C, F = (64, 1024, 512, 512)
        x = jax.random.normal(k0, (B, N, C), dtype=jnp.float32)
        W = jax.random.normal(k1, (C, F), dtype=jnp.float32) * (1.414 / np.sqrt(C + F))
        a = jax.random.normal(k2, (2 * F, 1), dtype=jnp.float32) * (1.414 / np.sqrt(2 * F + 1))
        beta = jnp.ones((1,), dtype=jnp.float32)
        mask = (jax.random.uniform(k3, (N, N)) < 0.3).astype(jnp.float32)
        return {'x': x, 'W': W, 'a': a, 'beta': beta, 'mask': mask}
    _L0_gnn_all = _L0_gnn_setup()
    _L0_gnn_in = {k: v for k, v in _L0_gnn_all.items() if k in ('W', 'a', 'beta', )}
    del _L0_gnn_all

    def _L1_gnn_setup():
        import jax, jax.numpy as jnp
        import numpy as np
        B, N, D, O = (8, 4096, 512, 512)
        key = jax.random.key(seed)
        k1, k2, k3, k4 = jax.random.split(key, 4)
        x = jax.random.normal(k1, (B, N, D), dtype=jnp.float32)
        adj = jax.random.uniform(k2, (N, N), dtype=jnp.float32)
        weight = jax.random.normal(k3, (D, O), dtype=jnp.float32) * 0.02
        bias = jax.random.normal(k4, (O,), dtype=jnp.float32) * 0.02
        return {'x': x, 'adj': adj, 'weight': weight, 'bias': bias}
    _L1_gnn_all = _L1_gnn_setup()
    _L1_gnn_in = {k: v for k, v in _L1_gnn_all.items() if k in ('weight', 'bias', )}
    del _L1_gnn_all

    return {
        "x": x,
        "adj": adj,
        "L0_gnn_W": _L0_gnn_in["W"],
        "L0_gnn_a": _L0_gnn_in["a"],
        "L0_gnn_beta": _L0_gnn_in["beta"],
        "L1_gnn_weight": _L1_gnn_in["weight"],
        "L1_gnn_bias": _L1_gnn_in["bias"],
    }

def reference(x, adj, L0_gnn_W, L0_gnn_a, L0_gnn_beta, L1_gnn_weight, L1_gnn_bias):
    import jax
    import jax.numpy as jnp
    def _L0_gnn_ref(x, W, a, beta, mask):
        import jax, jax.numpy as jnp
        import numpy as np
        ALPHA = 0.2
        F_ = W.shape[1]
        h = jnp.einsum('bnc,cf->bnf', x, W)
        a1, a2 = (a[:F_, 0], a[F_:, 0])
        s1 = jnp.einsum('bnf,f->bn', h, a1)
        s2 = jnp.einsum('bnf,f->bn', h, a2)
        e = jax.nn.leaky_relu(s1[:, :, None] + s2[:, None, :], negative_slope=ALPHA)
        e = e * mask[None, :, :]
        att = jax.nn.softmax(e, axis=2)
        h_prime = jnp.einsum('bij,bjf->bif', att, h)
        return jax.nn.elu(h_prime + beta * h)

    def _L1_gnn_ref(x, adj, weight, bias):
        import jax, jax.numpy as jnp
        import numpy as np
        B, N, D, O = (8, 4096, 512, 512)
        y = jnp.einsum('nm,bmd->bnd', adj, x)
        out = jnp.einsum('bnd,do->bno', y, weight) + bias
        return out

    h = jnp.maximum(_layernorm(x, axis=-1), 0.0)
    x = x + _L0_gnn_ref(h, L0_gnn_W, L0_gnn_a, L0_gnn_beta, adj)
    h = jnp.maximum(_layernorm(x, axis=-1), 0.0)
    x = x + _L1_gnn_ref(h, adj, L1_gnn_weight, L1_gnn_bias)
    return x


_drawn_inputs = setup_inputs


def setup_inputs(seed=0):
    import zlib

    import numpy as np

    out = dict(_drawn_inputs(seed))
    spreads = {}
    factors = {'L0_gnn_a': 8.0, 'L1_gnn_bias': 8.0}
    for name, (base, spread) in spreads.items():
        noise = np.random.default_rng([zlib.crc32(name.encode()), seed]).standard_normal(out[name].shape)
        drawn = base * np.exp(spread * noise) if base else spread * noise
        out[name] = jnp.asarray(drawn.astype(out[name].dtype))
    for name, factor in factors.items():
        out[name] = (out[name] * factor).astype(out[name].dtype)
    return out
```

```python
from contextlib import ExitStack

import concourse.bass as bass
from concourse import mybir

F32 = mybir.dt.float32
F16 = mybir.dt.float16
I32 = mybir.dt.int32
ALU = mybir.AluOpType
ACT = mybir.ActivationFunctionType
AX = mybir.AxisListType
ABSMAX = bass.bass_isa.ReduceOp.absmax

P = 128
SLOTS = 32
STAGES = 3
EPS = 1e-5
SLOPE = 0.2
HUGE = 3.0e38
TINY = 1.0e-30
EXPONENT = 0x7F800000
H_SCALE = 2.0 ** 11
TOP = 2.0 ** 14

LN0 = [0, 1, 2, 4, 6, 8, 10, 11]
TRANSPOSE = [21, 23, 26, 29, 36, 39, 42, 45]
PRE = [t - 4 for t in TRANSPOSE]
SPREAD = 15
RECIP = PRE[7] + 4
ATT = [32, 33, 34, 35, 52, 53, 54, 55]
GW = [48, 49, 50, 51, 60, 61, 62, 63]
Y = [68, 69, 70, 71, 72, 73, 74, 75]
OUT = [76, 77, 78, 79, 88, 89, 90, 91]
LOAD_X = [0, 0, 0, 0] + [t + 2 for t in LN0[:4]]
LOAD_ADJ = [8, 11] + [t + 2 for t in PRE[:6]]
RELOAD_X = [t - SLOTS + 1 for t in OUT]
BLOCKS = [("att", 0, 1), ("y", 0, 2), ("y", 1, 2), ("out", 0, 2), ("gw", 0, 1), ("att", 1, 1), ("out", 1, 2), ("gw", 1, 1)]


def tile_at(times, time):
    return times.index(time) if time in times else None


def tiles_at(times, time):
    return [n for n, t in enumerate(times) if t == time]


class Batch:

    def __init__(self, pair, offset):
        self.pair, self.offset = pair, offset
        self.number = 2 * pair + offset
        self.parity = offset % 2

    def count(self, per_batch, done):
        return (2 * per_batch) * self.pair + (per_batch * self.offset + done)

    def before(self):
        return Batch(self.pair, self.offset - 1)


def at_least(eng, sem, value):
    if not isinstance(value, int) or value > 0:
        eng.wait_ge(sem, value)


def two_layers(nc, x, adj, W, a, beta, weight, bias, out):
    B, N, C = x.shape
    T = N // P
    K = C // P
    HALF = N // 2
    TH = T // 2
    assert (T, K, W.shape[1], weight.shape[1]) == (8, 4, C, C)

    def live(pair, r):
        return {s: Batch(pair, r - s) for s in range(STAGES)}

    def run(eng, iteration):
        def edge(r):
            return {s: b for s, b in live(0, r).items() if 0 <= b.offset < B}
        for r in range(2):
            iteration(edge(r), edge(r - 1))
        with eng.Fori(0, (B - 2) // 2) as pair:
            for r in (2, 3):
                iteration(live(pair, r), live(pair, r - 1))
        for r in (B, B + 1):
            iteration(edge(r), edge(r - 1))

    with ExitStack() as ctx:
        def sb(name, shape, dt):
            return ctx.enter_context(nc.sbuf_tensor(name, shape, dt))

        def sem(name):
            return ctx.enter_context(nc.semaphore(name))

        ident = sb("ident", [P, P], F32)
        ones = sb("ones", [P, P], F32)
        minus_half = sb("minus_half", [P, 1], F32)
        betas = sb("betas", [P, 1], F32)
        peak = sb("peak", [P, 4], F32)
        peaks = sb("peaks", [P, 4], F32)
        bound = sb("bound", [P, 5], F32)
        pow2 = sb("pow2", [P, 5], F32)
        inv2 = sb("inv2", [P, 5], F32)
        scale = sb("scale", [P, 7], F32)
        w_scale, w2_scale, adj_scale, p_scale, g_scale, z_scale, o_scale = (scale[:, k:k + 1] for k in range(7))
        inexact = sb("inexact", [P, 1], I32)
        v_cols = sb("v_cols", [P, 2 * K], F32)
        v_rows = sb("v_rows", [P, 2, C], F32)
        bias_rows = sb("bias_rows", [P, C], F32)
        w_hi = sb("w_hi", [P, K, C], F16)
        w_lo = sb("w_lo", [P, K, C], F16)
        w2_hi = sb("w2_hi", [P, K, C], F16)
        w2_lo = sb("w2_lo", [P, K, C], F16)
        adjT_hi = sb("adjT_hi", [P, T, N], F16)
        adjT_lo = sb("adjT_lo", [P, T, N], F16)

        x_in = sb("x_in", [P, 4, C], F32)
        stats0 = sb("stats0", [P, T, 6], F32)
        mean0 = sb("mean0", [P, T, 2], F32)
        var0 = sb("var0", [P, T], F32)
        rstd0 = sb("rstd0", [P, T], F32)
        shift0 = sb("shift0", [P, T], F32)
        h0 = sb("h0", [P, 2, C], F32)
        h0_hi = sb("h0_hi", [P, 2, T, C], F16)
        h0_lo = sb("h0_lo", [P, 2, T, C], F16)
        junk = sb("junk", [P, 2, C], F16)
        s1 = sb("s1", [P, 2, T], F32)
        s2 = sb("s2", [P, T], F32)
        s2_diag = sb("s2_diag", [P, T, P], F32)
        s2_rows = sb("s2_rows", [P, N], F32)

        adj_in = sb("adj_in", [P, 2, N], F32)
        probs = sb("probs", [P, 2, N], F32)
        top = sb("top", [P, T], F32)
        minus_top = sb("minus_top", [P, T], F32)
        denom = sb("denom", [P, 2, T], F32)
        beta_denom = sb("beta_denom", [P, T], F32)
        inv_denom = sb("inv_denom", [P, T], F32)
        z_rows = sb("z_rows", [P, 2, T], F32)
        PT = sb("PT", [P, 2, T, N], F16)
        PT_hi, PT_lo = PT[:, 0], PT[:, 1]

        gT_hi = sb("gT_hi", [P, K, HALF], F16)
        gT_lo = sb("gT_lo", [P, K, HALF], F16)
        elu = sb("elu", [P, 2, C], F32)
        x1 = sb("x1", [P, T, C], F32)
        stats1 = sb("stats1", [P, T, 6], F32)
        mean1 = sb("mean1", [P, T, 2], F32)
        var1 = sb("var1", [P, T], F32)
        rstd1 = sb("rstd1", [P, T], F32)
        shift1 = sb("shift1", [P, T], F32)
        h1 = sb("h1", [P, 2, C], F32)
        h1_hi = sb("h1_hi", [P, T, C], F16)
        h1_lo = sb("h1_lo", [P, T, C], F16)

        yT_hi = sb("yT_hi", [P, K, N], F16)
        yT_lo = sb("yT_lo", [P, K, N], F16)

        W_in = probs[:, :, :].rearrange("p u n -> p (u n)")
        w2_in = x1[:, 0:K, :].rearrange("p k c -> p (k c)")
        a_rows = h1
        adj_all = PT[:, :, :, :].rearrange("p l t n -> p (l t n)").bitcast(F32).rearrange("p (t n) -> p t n", t=T)

        turned = [ctx.enter_context(nc.psum_tensor(f"turned{k}", [P, N], F32)) for k in range(2)]
        sums = [ctx.enter_context(nc.psum_tensor(f"sums{k}", [P, C], F32)) for k in range(4)]

        w_loaded = sem("w_loaded")
        w2_loaded = sem("w2_loaded")
        a_loaded = sem("a_loaded")
        bias_loaded = sem("bias_loaded")
        beta_loaded = sem("beta_loaded")
        adj_all_loaded = sem("adj_all_loaded")
        consts_ready = sem("consts_ready")
        v_cols_ready = sem("v_cols_ready")
        v_diag_ready = sem("v_diag_ready")
        v_spread = sem("v_spread")
        v_rows_ready = sem("v_rows_ready")
        peak_ready = sem("peak_ready")
        peaks_ready = sem("peaks_ready")
        scale_step = sem("scale_step")
        w_split = sem("w_split")
        adj_turned = sem("adj_turned")
        adjT_hi_ready = sem("adjT_hi_ready")
        adjT_lo_ready = sem("adjT_lo_ready")
        inexact_ready = sem("inexact_ready")

        x_loaded = [sem(f"x_loaded{k}") for k in range(4)]
        adj_loaded = [sem(f"adj_loaded{k}") for k in range(2)]
        x_reloaded = [sem(f"x_reloaded{k}") for k in range(T)]
        stored = [sem(f"stored{k}") for k in range(T)]
        stats0_taken = sem("stats0_taken")
        mean0_ready = sem("mean0_ready")
        var0_ready = sem("var0_ready")
        rstd0_ready = sem("rstd0_ready")
        shift0_ready = sem("shift0_ready")
        h0_ready = sem("h0_ready")
        h0_hi_ready = sem("h0_hi_ready")
        h0_lo_ready = sem("h0_lo_ready")
        s1_ready = sem("s1_ready")
        s2_ready = sem("s2_ready")
        s2_diag_ready = sem("s2_diag_ready")
        s2_spread = sem("s2_spread")
        s2_rows_ready = sem("s2_rows_ready")
        scores_ready = sem("scores_ready")
        leaky_ready = sem("leaky_ready")
        masked_ready = sem("masked_ready")
        minus_top_ready = sem("minus_top_ready")
        exp_ready = sem("exp_ready")
        beta_denom_ready = sem("beta_denom_ready")
        diag_added = sem("diag_added")
        inv_denom_ready = sem("inv_denom_ready")
        z_rows_ready = sem("z_rows_ready")
        probs_turned = sem("probs_turned")
        pT_hi_ready = sem("pT_hi_ready")
        pT_lo_ready = sem("pT_lo_ready")
        att_done = sem("att_done")
        gT_hi_ready = sem("gT_hi_ready")
        gT_lo_ready = sem("gT_lo_ready")
        gw_done = sem("gw_done")
        elu_exp_ready = sem("elu_exp_ready")
        elu_low_ready = sem("elu_low_ready")
        elu_ready = sem("elu_ready")
        x1_ready = sem("x1_ready")
        stats1_taken = sem("stats1_taken")
        mean1_ready = sem("mean1_ready")
        var1_ready = sem("var1_ready")
        rstd1_ready = sem("rstd1_ready")
        shift1_ready = sem("shift1_ready")
        h1_ready = sem("h1_ready")
        h1_hi_ready = sem("h1_hi_ready")
        h1_lo_ready = sem("h1_lo_ready")
        x1_bias_ready = sem("x1_bias_ready")
        y_done = sem("y_done")
        yT_hi_ready = sem("yT_hi_ready")
        yT_lo_ready = sem("yT_lo_ready")
        out_done = sem("out_done")
        result_ready = sem("result_ready")

        emptied = {"att": gT_lo_ready, "y": yT_lo_ready, "out": result_ready, "gw": elu_ready}

        def wait_apart(eng, *waits):
            waits = [(sem, value if isinstance(value, int) else eng.to_reg(value)) for sem, value in waits]
            eng.wait_ge(consts_ready, 4)
            for sem, value in waits:
                at_least(eng, sem, value)

        block = ctx.enter_context(nc.Block())

        @block.sync
        def _(sp):
            sp.dma_start(W_in.rearrange("p (k c) -> p k c", k=K), W.rearrange("(k p) c -> p k c", p=P)).then_inc(w_loaded, 16)
            for k in range(2):
                sp.dma_start(a_rows[:, k, :], a[k * C:(k + 1) * C, 0].partition_broadcast(P)).then_inc(a_loaded, 16)
            sp.dma_start(betas[:, :], beta.partition_broadcast(P)).then_inc(beta_loaded, 16)
            for t in range(T):
                sp.dma_start(adj_all[:, t, :], adj[t * P:(t + 1) * P, :]).then_inc(adj_all_loaded, 16)
            sp.dma_start(w2_in.rearrange("p (k c) -> p k c", k=K), weight.rearrange("(k p) c -> p k c", p=P)).then_inc(w2_loaded, 16)
            sp.dma_start(bias_rows[:, :], bias.partition_broadcast(P)).then_inc(bias_loaded, 16)

            def tile_of(tensor, b, n):
                return tensor[bass.ds(b.number, 1), n * P:(n + 1) * P, :].rearrange("o p c -> (o p) c")

            def step(b, time):
                for n in tiles_at(OUT, time):
                    sp.wait_ge(result_ready, b.count(T, n + 1))
                    sp.dma_start(tile_of(out, b, n), x1[:, n, :]).then_inc(stored[n], 16)
                for n in tiles_at(RELOAD_X, time):
                    at_least(sp, stored[n], b.count(16, 0))
                    if b.offset == 0:
                        sp.wait_ge(w_split, 4)
                    sp.dma_start(x1[:, n, :], tile_of(x, b, n)).then_inc(x_reloaded[n], 16)
                for n in tiles_at(LOAD_X, time):
                    at_least(sp, h0_ready, b.count(T, n + 1 - 4))
                    sp.dma_start(x_in[:, n % 4, :], tile_of(x, b, n)).then_inc(x_loaded[n % 4], 16)
                for n in tiles_at(LOAD_ADJ, time):
                    at_least(sp, masked_ready, b.count(T, n + 1 - 2))
                    sp.dma_start(adj_in[:, n % 2, :], adj[n * P:(n + 1) * P, :]).then_inc(adj_loaded[n % 2], 16)

            def iteration(batches, _):
                for slot in range(SLOTS):
                    for stage in sorted(batches, reverse=True):
                        step(batches[stage], SLOTS * stage + slot)

            run(sp, iteration)
            for n in range(T):
                sp.wait_ge(stored[n], 16 * B)

        @block.gpsimd
        def _(pool):
            pool.memset(ident[:, :], 0.0).then_inc(consts_ready, 1)
            pool.memset(ones[:, :], 1.0).then_inc(consts_ready, 1)
            pool.memset(minus_half[:, :], -0.5).then_inc(consts_ready, 1)
            pool.wait_ge(consts_ready, 1)
            pool.affine_select(out=ident[:, :], in_=ident[:, :], compare_op=ALU.not_equal, fill=1.0, base=0,
                               pattern=[[-1, P]], channel_multiplier=1).then_inc(consts_ready, 1)
            pool.wait_ge(consts_ready, 4)
            pool.wait_ge(v_cols_ready, 2 * K)
            for k in range(2 * K):
                pool.tensor_scalar(s2_diag[:, k, :], ident[:, :], v_cols[:, k:k + 1], None, ALU.mult)\
                    .then_inc(v_diag_ready, 1)
            pool.wait_ge(peak_ready, 3)
            pool.partition_all_reduce(peaks[:, 0:3], peak[:, 0:3], P, ABSMAX).then_inc(peaks_ready, 1)
            pool.wait_ge(peak_ready, 4)
            pool.partition_all_reduce(peaks[:, 3:4], peak[:, 3:4], P, ABSMAX).then_inc(peaks_ready, 1)
            pool.wait_ge(beta_loaded, 16)
            pool.wait_ge(bias_loaded, 16)

            def norm_scale(b, n, mean_sem, mean, var_sem, var, rstd_sem, rstd, shift_sem, shift):
                wait_apart(pool, (mean_sem, b.count(T, n + 1)))
                pool.tensor_scalar(var[:, n:n + 1], mean[:, n, 1:2], H_SCALE ** -2, EPS * H_SCALE ** -2,
                                   ALU.mult, ALU.add).then_inc(var_sem, 1)
                pool.wait_ge(var_sem, b.count(T, n + 1))
                pool.tensor_tensor(rstd[:, n:n + 1], var[:, n:n + 1], minus_half[:, :], ALU.pow).then_inc(rstd_sem, 1)
                wait_apart(pool, (rstd_sem, b.count(T, n + 1)))
                pool.tensor_scalar(shift[:, n:n + 1], mean[:, n, 0:1], rstd[:, n:n + 1], -1.0,
                                   ALU.mult, ALU.mult).then_inc(shift_sem, 1)

            def step(b, time):
                for n in tiles_at([t + 1 for t in GW], time):
                    norm_scale(b, n, mean1_ready, mean1, var1_ready, var1, rstd1_ready, rstd1, shift1_ready, shift1)
                for n in tiles_at([t + 1 for t in PRE], time):
                    wait_apart(pool, (masked_ready, b.count(T, n + 1)))
                    pool.tensor_scalar(minus_top[:, n:n + 1], top[:, n:n + 1], -1.0, None, ALU.mult)\
                        .then_inc(minus_top_ready, 1)
                for n in tiles_at([t + 2 for t in PRE], time):
                    wait_apart(pool, (exp_ready, b.count(T, n + 1)),
                                     (diag_added, b.count(T, n + 1 - T)))
                    pool.tensor_scalar(beta_denom[:, n:n + 1], denom[:, b.parity, n:n + 1], betas[:, 0:1], None, ALU.mult)\
                        .then_inc(beta_denom_ready, 1)
                for n in tiles_at(LN0, time):
                    norm_scale(b, n, mean0_ready, mean0, var0_ready, var0, rstd0_ready, rstd0, shift0_ready, shift0)
                for n in tiles_at([t + 3 for t in LN0], time):
                    if b.offset == 0:
                        pool.wait_ge(v_spread, 1)
                    wait_apart(pool, (s2_ready, b.count(T, n + 1)),
                                     (s2_spread, b.count(1, 0)))
                    pool.tensor_scalar(s2_diag[:, n, :], ident[:, :], s2[:, n:n + 1], None, ALU.mult)\
                        .then_inc(s2_diag_ready, 1)
                for n in tiles_at([t + 3 for t in GW], time):
                    pool.wait_ge(h1_hi_ready, b.count(T, n + 1))
                    at_least(pool, y_done, b.count(T, 0))
                    pool.tensor_tensor(h1_lo[:, n, :], h1[:, n % 2, :], h1_hi[:, n, :], ALU.subtract)\
                        .then_inc(h1_lo_ready, 1)
                    pool.tensor_tensor(x1[:, n, :], x1[:, n, :], bias_rows[:, :], ALU.add).then_inc(x1_bias_ready, 1)
                for n in tiles_at([t + 2 for t in LN0], time):
                    pool.wait_ge(h0_hi_ready, b.count(T, n + 1))
                    at_least(pool, att_done, b.count(T, -T))
                    pool.tensor_tensor(h0_lo[:, b.parity, n, :], h0[:, n % 2, :], h0_hi[:, b.parity, n, :], ALU.subtract)\
                        .then_inc(h0_lo_ready, 1)

            def group(b, time):
                for n in tiles_at(GW, time):
                    pool.wait_ge(elu_ready, b.count(T, n + 1))
                    pool.wait_ge(x_reloaded[n], b.count(16, 16))
                    pool.tensor_tensor(x1[:, n, :], x1[:, n, :], elu[:, n % 2, :], ALU.add).then_inc(x1_ready, 1)

            def iteration(batches, _):
                for slot in range(SLOTS):
                    for stage in sorted(batches, reverse=True):
                        step(batches[stage], SLOTS * stage + slot)
                    for stage in batches:
                        group(batches[stage], SLOTS * stage + slot)

            run(pool, iteration)

        @block.scalar
        def _(act):
            act.wait_ge(v_spread, 1)
            act.activation(v_rows[:, :, :].rearrange("p k c -> p (k c)"), turned[0][:, :], ACT.Copy).then_inc(v_rows_ready, 1)
            act.wait_ge(scale_step, 13)
            for t in range(T):
                act.wait_ge(adj_turned, t + 1)
                act.activation(adjT_hi[:, :, t * P:(t + 1) * P], turned[(t + 1) % 2][:, :].rearrange("p (t i) -> p t i", t=T),
                               ACT.Copy, scale=adj_scale).then_inc(adjT_hi_ready, 1)

            def step(b, time):
                for n in tiles_at([t + 1 for t in TRANSPOSE], time):
                    act.wait_ge(probs_turned, b.count(T, n + 1))
                    act.activation(PT_hi[:, :, n * P:(n + 1) * P], turned[n % 2][:, :].rearrange("p (t i) -> p t i", t=T),
                                   ACT.Copy, scale=p_scale).then_inc(pT_hi_ready, 1)
                for n in tiles_at([t + 2 for t in PRE], time):
                    act.wait_ge(minus_top_ready, b.count(T, n + 1))
                    act.activation(probs[:, n % 2, :], probs[:, n % 2, :], ACT.Exp, bias=minus_top[:, n:n + 1],
                                   accum_out=denom[:, b.parity, n:n + 1]).then_inc(exp_ready, 1)
                for n in tiles_at([t + 2 for t in GW], time):
                    act.wait_ge(shift1_ready, b.count(T, n + 1))
                    at_least(act, h1_lo_ready, b.count(T, n + 1 - 2))
                    act.activation(h1[:, n % 2, :], x1[:, n, :], ACT.Relu, bias=shift1[:, n:n + 1],
                                   scale=rstd1[:, n:n + 1]).then_inc(h1_ready, 1)
                for n in tiles_at([t + 1 for t in LN0], time):
                    act.wait_ge(shift0_ready, b.count(T, n + 1))
                    at_least(act, h0_lo_ready, b.count(T, n + 1 - 2))
                    at_least(act, s2_ready, b.count(T, n + 1 - 2))
                    act.activation(h0[:, n % 2, :], x_in[:, n % 4, :], ACT.Relu, bias=shift0[:, n:n + 1],
                                   scale=rstd0[:, n:n + 1]).then_inc(h0_ready, 1)
                if time == SPREAD + 1:
                    act.wait_ge(s2_spread, b.count(1, 1))
                    at_least(act, scores_ready, b.count(T, 0))
                    act.activation(s2_rows[:, :], turned[0][:, :], ACT.Copy).then_inc(s2_rows_ready, 1)
                for n in tiles_at(PRE, time):
                    act.wait_ge(s2_rows_ready, b.count(1, 1))
                    act.wait_ge(s1_ready, b.count(T, n + 1))
                    at_least(act, probs_turned, b.count(T, n + 1 - 2))
                    if b.offset == 0:
                        act.wait_ge(w_split, 2)
                    act.activation(probs[:, n % 2, :], s2_rows[:, :], ACT.Identity, bias=s1[:, b.parity, n:n + 1])\
                        .then_inc(scores_ready, 1)

            def group(b, time):
                for n in tiles_at(ATT, time):
                    half, c = divmod(n, K)
                    act.wait_ge(att_done, b.count(T, n + 1))
                    act.activation(gT_hi[:, c, :], sums[c][:, :], ACT.Copy, scale=g_scale).then_inc(gT_hi_ready, 1)
                for n in tiles_at(GW, time):
                    act.wait_ge(gw_done, b.count(T, n + 1))
                    act.wait_ge(z_rows_ready, b.count(1, 1))
                    at_least(act, x1_ready, b.count(T, n + 1 - 2))
                    act.activation(elu[:, n % 2, :], sums[n % 4][:, :], ACT.Exp, scale=z_rows[:, b.parity, n:n + 1])\
                        .then_inc(elu_exp_ready, 1)
                for n in tiles_at(Y, time):
                    half, d = divmod(n, K)
                    act.wait_ge(y_done, b.count(T, n + 1))
                    act.activation(yT_hi[:, d, half * HALF:(half + 1) * HALF], sums[d][:, :], ACT.Copy,
                                   scale=1.0 / (TOP * H_SCALE)).then_inc(yT_hi_ready, 1)

            def iteration(batches, _):
                for slot in range(SLOTS):
                    for stage in sorted(batches, reverse=True):
                        step(batches[stage], SLOTS * stage + slot)
                    for stage in batches:
                        group(batches[stage], SLOTS * stage + slot)

            run(act, iteration)

        @block.vector
        def _(dve):
            dve.wait_ge(w_loaded, 16)
            dve.wait_ge(a_loaded, 32)
            for k in range(2 * K):
                if k >= 2:
                    dve.wait_ge(v_cols_ready, k - 1)
                dve.tensor_tensor_reduce(junk[:, k % 2, :], W_in[:, (k % K) * C:(k % K + 1) * C], a_rows[:, k // K, :],
                                         1.0 / H_SCALE, 0.0, ALU.mult, ALU.add, v_cols[:, k:k + 1]).then_inc(v_cols_ready, 1)
            dve.tensor_reduce(peak[:, 0:1], W_in, AX.X, ALU.max, apply_absolute_value=True).then_inc(peak_ready, 1)
            dve.wait_ge(w2_loaded, 16)
            dve.tensor_reduce(peak[:, 1:2], w2_in, AX.X, ALU.max, apply_absolute_value=True).then_inc(peak_ready, 1)
            dve.wait_ge(adj_all_loaded, 16 * T)
            dve.tensor_reduce(peak[:, 2:3], adj_all.rearrange("p t n -> p (t n)"), AX.X, ALU.max,
                              apply_absolute_value=True).then_inc(peak_ready, 1)
            dve.wait_ge(beta_loaded, 16)
            dve.scalar_tensor_tensor(bound[:, 4:5], betas[:, :], -1.0, betas[:, :], ALU.mult, ALU.max).then_inc(scale_step, 1)
            dve.wait_ge(scale_step, 1)
            dve.tensor_scalar(bound[:, 3:4], bound[:, 4:5], float(N), 1.0, ALU.mult, ALU.add).then_inc(scale_step, 1)
            dve.wait_ge(scale_step, 2)
            dve.tensor_scalar(bound[:, 4:5], bound[:, 4:5], 1.0, None, ALU.add).then_inc(scale_step, 1)
            dve.wait_ge(peaks_ready, 1)
            dve.tensor_scalar(bound[:, 0:3], peaks[:, 0:3], TINY, None, ALU.max).then_inc(scale_step, 1)
            dve.wait_ge(scale_step, 4)
            dve.tensor_scalar(pow2[:, :].bitcast(I32), bound[:, :].bitcast(I32), EXPONENT, None, ALU.bitwise_and)\
                .then_inc(scale_step, 1)
            dve.wait_ge(scale_step, 5)
            dve.reciprocal(inv2[:, :], pow2[:, :]).then_inc(scale_step, 1)
            dve.wait_ge(scale_step, 6)
            dve.tensor_scalar(scale[:, 0:4], inv2[:, 0:4], TOP, None, ALU.mult).then_inc(scale_step, 1)
            dve.tensor_scalar(bound[:, 0:1], pow2[:, 3:4], 1.0 / (H_SCALE * TOP), None, ALU.mult).then_inc(scale_step, 1)
            dve.tensor_scalar(bound[:, 1:2], pow2[:, 4:5], 1.0 / TOP, None, ALU.mult).then_inc(scale_step, 1)
            dve.tensor_scalar(bound[:, 2:3], pow2[:, 2:3], 1.0 / TOP, None, ALU.mult).then_inc(scale_step, 1)
            dve.wait_ge(scale_step, 10)
            dve.tensor_tensor(g_scale, bound[:, 0:1], inv2[:, 4:5], ALU.mult).then_inc(scale_step, 1)
            dve.tensor_tensor(z_scale, bound[:, 1:2], pow2[:, 0:1], ALU.mult).then_inc(scale_step, 1)
            dve.tensor_tensor(o_scale, bound[:, 2:3], pow2[:, 1:2], ALU.mult).then_inc(scale_step, 1)
            dve.wait_ge(scale_step, 13)
            for step_at, (whole, factor, hi, lo) in enumerate([(W_in, w_scale, w_hi, w_lo), (w2_in, w2_scale, w2_hi, w2_lo)]):
                dve.tensor_scalar(whole, whole, factor, None, ALU.mult).then_inc(scale_step, 1)
                dve.wait_ge(scale_step, 14 + step_at)
                dve.tensor_copy(hi[:, :, :].rearrange("p k c -> p (k c)"), whole).then_inc(w_split, 1)
                dve.wait_ge(w_split, 2 * step_at + 1)
                dve.tensor_tensor(lo[:, :, :].rearrange("p k c -> p (k c)"), whole, hi[:, :, :].rearrange("p k c -> p (k c)"),
                                  ALU.subtract).then_inc(w_split, 1)
            for t in range(T):
                dve.wait_ge(adjT_hi_ready, t + 1)
                dve.scalar_tensor_tensor(adjT_lo[:, :, t * P:(t + 1) * P], turned[(t + 1) % 2][:, :].rearrange("p (t i) -> p t i", t=T),
                                         adj_scale, adjT_hi[:, :, t * P:(t + 1) * P], ALU.mult, ALU.subtract)\
                    .then_inc(adjT_lo_ready, 1)
            dve.wait_ge(adjT_lo_ready, T)
            dve.tensor_reduce(peak[:, 3:4], adjT_lo[:, :, :].rearrange("p t n -> p (t n)"), AX.X, ALU.max,
                              apply_absolute_value=True).then_inc(peak_ready, 1)
            dve.wait_ge(peaks_ready, 2)
            dve.tensor_scalar(inexact[:, :], peaks[:, 3:4], 0.0, None, ALU.is_gt).then_inc(inexact_ready, 1)
            dve.wait_ge(v_rows_ready, 1)

            def step(b, time):
                for n in tiles_at([t + 1 for t in TRANSPOSE], time):
                    dve.wait_ge(pT_hi_ready, b.count(T, n + 1))
                    dve.scalar_tensor_tensor(PT_lo[:, :, n * P:(n + 1) * P], turned[n % 2][:, :].rearrange("p (t i) -> p t i", t=T),
                                             p_scale, PT_hi[:, :, n * P:(n + 1) * P], ALU.mult, ALU.subtract)\
                        .then_inc(pT_lo_ready, 1)
                for n in tiles_at([t + 3 for t in PRE], time):
                    own = probs[:, n % 2, n * P:(n + 1) * P]
                    dve.wait_ge(beta_denom_ready, b.count(T, n + 1))
                    dve.scalar_tensor_tensor(own, ident[:, :], beta_denom[:, n:n + 1], own, ALU.mult, ALU.add)\
                        .then_inc(diag_added, 1)
                if time == RECIP:
                    dve.wait_ge(exp_ready, b.count(T, T))
                    at_least(dve, z_rows_ready, b.count(1, 0))
                    dve.reciprocal(inv_denom[:, :], denom[:, b.parity, :]).then_inc(inv_denom_ready, 1)
                    dve.wait_ge(inv_denom_ready, b.count(1, 1))
                    dve.tensor_scalar(z_rows[:, b.parity, :], inv_denom[:, :], z_scale, None, ALU.mult).then_inc(z_rows_ready, 1)
                for n in tiles_at([t + 3 for t in GW], time):
                    dve.wait_ge(h1_ready, b.count(T, n + 1))
                    at_least(dve, y_done, b.count(T, 0))
                    dve.tensor_copy(h1_hi[:, n, :], h1[:, n % 2, :]).then_inc(h1_hi_ready, 1)
                for n in tiles_at([t + 1 for t in GW], time):
                    dve.wait_ge(x1_ready, b.count(T, n + 1))
                    dve.bn_stats(stats1[:, n, :], x1[:, n, :]).then_inc(stats1_taken, 1)
                    wait_apart(dve, (stats1_taken, b.count(T, n + 1)))
                    dve.bn_aggr(mean1[:, n, :], stats1[:, n, :]).then_inc(mean1_ready, 1)
                for n in tiles_at([t + 1 for t in PRE], time):
                    own = probs[:, n % 2, :]
                    dve.wait_ge(scores_ready, b.count(T, n + 1))
                    dve.scalar_tensor_tensor(own, own, SLOPE, own, ALU.mult, ALU.max).then_inc(leaky_ready, 1)
                    wait_apart(dve, (leaky_ready, b.count(T, n + 1)),
                                    (adj_loaded[n % 2], b.count(64, 16 * (n // 2 + 1))))
                    dve.tensor_tensor_reduce(own, own, adj_in[:, n % 2, :], 1.0, -HUGE, ALU.mult, ALU.max, top[:, n:n + 1])\
                        .then_inc(masked_ready, 1)
                for n in tiles_at([t + 2 for t in LN0], time):
                    dve.wait_ge(h0_ready, b.count(T, n + 1))
                    at_least(dve, att_done, b.count(T, -T))
                    dve.tensor_copy(h0_hi[:, b.parity, n, :], h0[:, n % 2, :]).then_inc(h0_hi_ready, 1)
                    at_least(dve, s1_ready, b.count(T, n))
                    dve.tensor_tensor_reduce(junk[:, 0, :], h0[:, n % 2, :], v_rows[:, 0, :], 1.0, 0.0, ALU.mult, ALU.add,
                                             s1[:, b.parity, n:n + 1]).then_inc(s1_ready, 1)
                    at_least(dve, s2_ready, b.count(T, n))
                    dve.tensor_tensor_reduce(junk[:, 1, :], h0[:, n % 2, :], v_rows[:, 1, :], 1.0, 0.0, ALU.mult, ALU.add,
                                             s2[:, n:n + 1]).then_inc(s2_ready, 1)
                for n in tiles_at(LN0, time):
                    dve.wait_ge(x_loaded[n % 4], b.count(32, 16 * (n // 4 + 1)))
                    dve.bn_stats(stats0[:, n, :], x_in[:, n % 4, :]).then_inc(stats0_taken, 1)
                    wait_apart(dve, (stats0_taken, b.count(T, n + 1)))
                    dve.bn_aggr(mean0[:, n, :], stats0[:, n, :]).then_inc(mean0_ready, 1)

            def group(b, time):
                for n in tiles_at(ATT, time):
                    c = n % K
                    dve.wait_ge(gT_hi_ready, b.count(T, n + 1))
                    dve.scalar_tensor_tensor(gT_lo[:, c, :], sums[c][:, :], g_scale, gT_hi[:, c, :], ALU.mult, ALU.subtract)\
                        .then_inc(gT_lo_ready, 1)
                for n in tiles_at(GW, time):
                    own = elu[:, n % 2, :]
                    dve.wait_ge(elu_exp_ready, b.count(T, n + 1))
                    dve.tensor_scalar(own, own, 1.0, -1.0, ALU.min, ALU.add).then_inc(elu_low_ready, 1)
                    dve.wait_ge(elu_low_ready, b.count(T, n + 1))
                    dve.scalar_tensor_tensor(own, sums[n % 4][:, :], z_rows[:, b.parity, n:n + 1], own, ALU.mult, ALU.max)\
                        .then_inc(elu_ready, 1)
                for n in tiles_at(Y, time):
                    half, d = divmod(n, K)
                    dve.wait_ge(yT_hi_ready, b.count(T, n + 1))
                    dve.scalar_tensor_tensor(yT_lo[:, d, half * HALF:(half + 1) * HALF], sums[d][:, :], 1.0 / (TOP * H_SCALE),
                                             yT_hi[:, d, half * HALF:(half + 1) * HALF], ALU.mult, ALU.subtract)\
                        .then_inc(yT_lo_ready, 1)
                for n in tiles_at(OUT, time):
                    dve.wait_ge(out_done, b.count(T, n + 1))
                    dve.wait_ge(x1_bias_ready, b.count(T, n + 1))
                    dve.scalar_tensor_tensor(x1[:, n, :], sums[n % 4][:, :], o_scale, x1[:, n, :], ALU.mult, ALU.add)\
                        .then_inc(result_ready, 1)

            def iteration(batches, _):
                for slot in range(SLOTS):
                    for stage in sorted(batches, reverse=True):
                        step(batches[stage], SLOTS * stage + slot)
                    for stage in batches:
                        group(batches[stage], SLOTS * stage + slot)

            run(dve, iteration)

        @block.tensor
        def _(pe):
            def spread(diags, sem_done):
                for k in range(T):
                    last = pe.matmul(turned[0][:, k * P:(k + 1) * P], ones[:, :], diags[:, k, :], start=True, stop=True)
                last.then_inc(sem_done, 1)

            def turn(rows, into, sem_done):
                for k in range(T):
                    last = pe.transpose(into[:, k * P:(k + 1) * P], rows[:, k * P:(k + 1) * P], ident[:, :])
                last.then_inc(sem_done, 1)

            pe.wait_ge(v_diag_ready, 2 * K)
            pe.wait_ge(consts_ready, 4)
            spread(s2_diag, v_spread)
            pe.wait_ge(adj_all_loaded, 16 * T)
            for t in range(T):
                if t >= 2:
                    pe.wait_ge(adjT_lo_ready, t - 1)
                elif t == 1:
                    pe.wait_ge(v_rows_ready, 1)
                turn(adj_all[:, t, :], turned[(t + 1) % 2], adj_turned)
            pe.wait_ge(inexact_ready, 1)
            adj_has_low = pe.value_load(inexact[0:1, 0:1], min_val=0, max_val=1)
            pe.wait_ge(w_split, 4)
            pe.wait_ge(adjT_lo_ready, T)

            def bank_free(k, i, batches, last_batches):
                for back in range(1, len(BLOCKS)):
                    kind, half, stage = BLOCKS[k - back]
                    present = batches if back <= k else last_batches
                    if stage in present:
                        at_least(pe, emptied[kind], present[stage].count(T, TH * half + i + 1))
                        return

            def products(bank, pairs):
                for j, (stationary, moving) in enumerate(pairs):
                    last = pe.matmul(bank, stationary, moving, start=(j == 0), stop=(j == len(pairs) - 1))
                return last

            def group(b, time, batches, last_batches):
                bank_free((time % SLOTS) // TH, time % TH, batches, last_batches)
                for n in tiles_at(ATT, time):
                    half, c = divmod(n, K)
                    cols, rows = slice(c * P, (c + 1) * P), slice(half * HALF, (half + 1) * HALF)
                    if c == 0:
                        pe.wait_ge(pT_lo_ready, b.count(T, TH * (half + 1)))
                        pe.wait_ge(h0_lo_ready, b.count(T, T))
                    products(sums[c][:, :], [
                        pair for j in range(T) for pair in (
                            (h0_hi[:, b.parity, j, cols], PT_hi[:, j, rows]),
                            (h0_hi[:, b.parity, j, cols], PT_lo[:, j, rows]),
                            (h0_lo[:, b.parity, j, cols], PT_hi[:, j, rows]))
                    ]).then_inc(att_done, 1)
                for n in tiles_at(GW, time):
                    rows = slice((n % TH) * P, (n % TH + 1) * P)
                    pe.wait_ge(gT_lo_ready, b.count(T, TH * (n // TH + 1)))
                    products(sums[n % 4][:, :], [
                        pair for c in range(K) for pair in (
                            (gT_hi[:, c, rows], w_hi[:, c, :]),
                            (gT_hi[:, c, rows], w_lo[:, c, :]),
                            (gT_lo[:, c, rows], w_hi[:, c, :]))
                    ]).then_inc(gw_done, 1)
                for n in tiles_at(Y, time):
                    half, d = divmod(n, K)
                    cols, rows = slice(d * P, (d + 1) * P), slice(half * HALF, (half + 1) * HALF)
                    if n == 0:
                        pe.wait_ge(h1_lo_ready, b.count(T, T))
                    bank = sums[d][:, :]
                    pe.matmul(bank, h1_hi[:, 0, cols], adjT_hi[:, 0, rows], start=True, stop=False)
                    with pe.If(adj_has_low > 0):
                        for j in range(T):
                            pe.matmul(bank, h1_hi[:, j, cols], adjT_lo[:, j, rows], start=False, stop=False)
                    for j in range(1, T):
                        pe.matmul(bank, h1_hi[:, j, cols], adjT_hi[:, j, rows], start=False, stop=False)
                    for j in range(T):
                        last = pe.matmul(bank, h1_lo[:, j, cols], adjT_hi[:, j, rows], start=False, stop=(j == T - 1))
                    last.then_inc(y_done, 1)
                for n in tiles_at(OUT, time):
                    rows = slice(n * P, (n + 1) * P)
                    pe.wait_ge(yT_lo_ready, b.count(T, TH * (n // TH + 1)))
                    products(sums[n % 4][:, :], [
                        pair for d in range(K) for pair in (
                            (yT_hi[:, d, rows], w2_hi[:, d, :]),
                            (yT_hi[:, d, rows], w2_lo[:, d, :]),
                            (yT_lo[:, d, rows], w2_hi[:, d, :]))
                    ]).then_inc(out_done, 1)

            def step(b, time):
                if time == SPREAD:
                    pe.wait_ge(s2_diag_ready, b.count(T, T))
                    at_least(pe, pT_lo_ready, b.count(T, T - 1 - T))
                    spread(s2_diag, s2_spread)
                for n in tiles_at(TRANSPOSE, time):
                    pe.wait_ge(diag_added, b.count(T, n + 1))
                    if n == 0:
                        pe.wait_ge(s2_rows_ready, b.count(1, 1))
                    else:
                        at_least(pe, pT_lo_ready, b.count(T, n - 1))
                    turn(probs[:, n % 2, :], turned[n % 2], probs_turned)

            def iteration(batches, last_batches):
                for slot in range(SLOTS):
                    for stage in batches:
                        time = SLOTS * stage + slot
                        if time in ATT + GW + Y + OUT:
                            group(batches[stage], time, batches, last_batches)
                    for stage in sorted(batches, reverse=True):
                        step(batches[stage], SLOTS * stage + slot)

            run(pe, iteration)


_INS = ["x", "adj", "L0_gnn_W", "L0_gnn_a", "L0_gnn_beta", "L1_gnn_weight", "L1_gnn_bias"]
_OUTS = [((16, 1024, 512), "float32")]


def kernel(**inputs):
    import numpy as _np
    import concourse.bacc as _bacc
    from concourse import mybir as _mybir
    from concourse.bass_utils import run_bass_kernel_spmd as _run

    nc = _bacc.Bacc("TRN2", target_bir_lowering=False, num_devices=1, dynamic_dma_scratch_size=1024)
    arrays, args = {}, []
    for name in _INS:
        a = _np.ascontiguousarray(inputs[name])
        arrays[f"in_{name}_dram"] = a
        args.append(nc.dram_tensor(f"in_{name}_dram", a.shape, _mybir.dt.from_np(a.dtype), kind="ExternalInput").ap())
    for i, (shape, dtype) in enumerate(_OUTS):
        dt = _mybir.dt.from_np(_np.dtype(dtype))
        args.append(nc.dram_tensor(f"out_{i}_dram", shape, dt, kind="ExternalOutput").ap())
    two_layers(nc, *args)
    r = _run(nc, [arrays], core_ids=[0])
    return r.results[0]["out_0_dram"]
```

```python
from contextlib import ExitStack

import concourse.bass as bass
from concourse import mybir

F32 = mybir.dt.float32
F16 = mybir.dt.float16
I32 = mybir.dt.int32
ALU = mybir.AluOpType
ACT = mybir.ActivationFunctionType
AX = mybir.AxisListType
ABSMAX = bass.bass_isa.ReduceOp.absmax

P = 128
SLOTS = 32
STAGES = 3
EPS = 1e-5
SLOPE = 0.2
HUGE = 3.0e38
TINY = 1.0e-30
EXPONENT = 0x7F800000
H_SCALE = 2.0 ** 11
TOP = 2.0 ** 14
Y_SCALE = 2.0 ** 10

NORM0 = [0, 0, 1, 2, 4, 6, 8, 9]
H0 = [1, 2, 3, 5, 7, 9, 11, 12]
SPREAD = [6, 7, 8, 10, 12, 14, 16, 17]
PRE = [18, 20, 22, 24, 34, 36, 38, 40]
RECIP = PRE[7] + 4
ATT = [32, 33, 34, 35, 52, 53, 54, 55]
GW = [48, 49, 50, 51, 60, 61, 62, 63]
Y = [68, 69, 70, 71, 72, 73, 74, 75]
OUT = [76, 77, 78, 79, 88, 89, 90, 91]
SUM_ADJ = [0, 1, 2, 3, 4, 5, 6, 7]
SUM_W = [1, 5]
SCALES = 13
SPLIT = [29, 37]
PARTS = [t + 1 for t in PRE]
INEXACT = PARTS[7] + 4
LOAD_X = [0, 0, 0, 0] + [t + 1 for t in H0[:4]]
LOAD_ADJ = [8, 11] + [t + 2 for t in PRE[:6]]
RELOAD_X = [t - SLOTS + 1 for t in OUT]
BLOCKS = [("att", 0, 1), ("y", 0, 2), ("y", 1, 2), ("out", 0, 2), ("gw", 0, 1), ("att", 1, 1), ("out", 1, 2), ("gw", 1, 1)]


def tile_at(times, time):
    return times.index(time) if time in times else None


def tiles_at(times, time):
    return [n for n, t in enumerate(times) if t == time]


class Batch:

    def __init__(self, pair, offset):
        self.pair, self.offset = pair, offset
        self.number = 2 * pair + offset
        self.parity = offset % 2

    def count(self, per_batch, done):
        return (2 * per_batch) * self.pair + (per_batch * self.offset + done)

    def before(self):
        return Batch(self.pair, self.offset - 1)

    @property
    def first(self):
        return isinstance(self.number, int) and self.number == 0

    @property
    def second(self):
        return isinstance(self.number, int) and self.number == 1


def at_least(eng, sem, value):
    if not isinstance(value, int) or value > 0:
        eng.wait_ge(sem, value)


def two_layers(nc, x, adj, W, a, beta, weight, bias, out):
    B, N, C = x.shape
    T = N // P
    K = C // P
    HALF = N // 2
    TH = T // 2
    assert (T, K, W.shape[1], weight.shape[1]) == (8, 4, C, C)

    def live(pair, r):
        return {s: Batch(pair, r - s) for s in range(STAGES)}

    def run(eng, iteration, before_loop=None):
        def edge(r):
            return {s: b for s, b in live(0, r).items() if 0 <= b.offset < B}
        for r in range(2):
            iteration(edge(r), edge(r - 1))
        if before_loop:
            before_loop()
        with eng.Fori(0, (B - 2) // 2) as pair:
            for r in (2, 3):
                iteration(live(pair, r), live(pair, r - 1))
        for r in (B, B + 1):
            iteration(edge(r), edge(r - 1))

    with ExitStack() as ctx:
        def sb(name, shape, dt):
            return ctx.enter_context(nc.sbuf_tensor(name, shape, dt))

        def sem(name):
            return ctx.enter_context(nc.semaphore(name))

        ident = sb("ident", [P, P], F32)
        ones = sb("ones", [P, P], F32)
        minus_half = sb("minus_half", [P, 1], F32)
        betas = sb("betas", [P, 1], F32)
        adj_sums = sb("adj_sums", [P, T], F32)
        low_sums = sb("low_sums", [P, T], F32)
        peak = sb("peak", [P, 4], F32)
        peaks = sb("peaks", [P, 4], F32)
        bound = sb("bound", [P, 5], F32)
        pow2 = sb("pow2", [P, 5], F32)
        inv2 = sb("inv2", [P, 5], F32)
        scale = sb("scale", [P, 7], F32)
        w_scale, w2_scale, adj_scale, p_scale, g_scale, z_scale, o_scale = (scale[:, k:k + 1] for k in range(7))
        inexact = sb("inexact", [P, 1], I32)
        v_cols = sb("v_cols", [P, 2 * K], F32)
        v_rows = sb("v_rows", [P, 2, C], F32)
        bias_rows = sb("bias_rows", [P, C], F32)
        w_hi = sb("w_hi", [P, K, C], F16)
        w_lo = sb("w_lo", [P, K, C], F16)
        w2_hi = sb("w2_hi", [P, K, C], F16)
        w2_lo = sb("w2_lo", [P, K, C], F16)
        adjT_hi = sb("adjT_hi", [P, T, N], F16)
        adjT_lo = sb("adjT_lo", [P, T, N], F16)

        x_in = sb("x_in", [P, 4, C], F32)
        stats0 = sb("stats0", [P, T, 6], F32)
        mean0 = sb("mean0", [P, T, 2], F32)
        var0 = sb("var0", [P, T], F32)
        rstd0 = sb("rstd0", [P, T], F32)
        shift0 = sb("shift0", [P, T], F32)
        h0 = sb("h0", [P, 2, C], F32)
        h0_hi = sb("h0_hi", [P, 2, T, C], F16)
        h0_lo = sb("h0_lo", [P, 2, T, C], F16)
        junk = sb("junk", [P, C], F16)
        s1 = sb("s1", [P, 2, T], F32)
        s2 = sb("s2", [P, T], F32)
        s2_diag = sb("s2_diag", [P, 2, P], F32)

        adj_in = sb("adj_in", [P, 2, N], F32)
        probs = sb("probs", [P, 2, N], F32)
        top = sb("top", [P, T], F32)
        minus_top = sb("minus_top", [P, T], F32)
        denom = sb("denom", [P, 2, T], F32)
        beta_denom = sb("beta_denom", [P, T], F32)
        inv_denom = sb("inv_denom", [P, T], F32)
        z_rows = sb("z_rows", [P, 2, T], F32)
        rows_hi = sb("rows_hi", [P, 2, N], F16)
        rows_lo = sb("rows_lo", [P, 2, N], F16)
        PT = sb("PT", [P, 2, T, N], F16)
        PT_hi, PT_lo = PT[:, 0], PT[:, 1]

        gT_hi = sb("gT_hi", [P, K, HALF], F16)
        gT_lo = sb("gT_lo", [P, K, HALF], F16)
        elu = sb("elu", [P, 2, C], F32)
        x1 = sb("x1", [P, T, C], F32)
        stats1 = sb("stats1", [P, T, 6], F32)
        mean1 = sb("mean1", [P, T, 2], F32)
        var1 = sb("var1", [P, T], F32)
        rstd1 = sb("rstd1", [P, T], F32)
        shift1 = sb("shift1", [P, T], F32)
        h1 = sb("h1", [P, 2, C], F32)
        h1_hi = sb("h1_hi", [P, T, C], F16)
        h1_lo = sb("h1_lo", [P, T, C], F16)

        yT_hi = sb("yT_hi", [P, K, N], F16)
        yT_lo = sb("yT_lo", [P, K, N], F16)

        W_in = x1[:, 0:K, :].rearrange("p k c -> p (k c)")
        w2_in = x1[:, K:2 * K, :].rearrange("p k c -> p (k c)")
        a_rows = h1
        v_diag = rows_hi[:, :, :].rearrange("p u n -> p (u n)").bitcast(F32).rearrange("p (k i) -> p k i", k=2 * K)
        abs_w = probs[:, :, :].rearrange("p u n -> p (u n)")
        adj_rows_hi, adj_rows_lo = (yT[:, :, :] for yT in (yT_hi, yT_lo))
        abs_low = h1_lo[:, :, :].rearrange("p (k u) c -> p k (u c)", k=4)

        s2_rows = [ctx.enter_context(nc.psum_tensor(f"s2_rows{k}", [P, N], F32)) for k in range(2)]
        sums = [ctx.enter_context(nc.psum_tensor(f"sums{k}", [P, C], F32)) for k in range(4)]

        w_loaded = [sem(f"w_loaded{k}") for k in range(K)]
        w2_loaded = sem("w2_loaded")
        a_loaded = sem("a_loaded")
        bias_loaded = sem("bias_loaded")
        beta_loaded = sem("beta_loaded")
        consts_ready = sem("consts_ready")
        v_cols_ready = sem("v_cols_ready")
        v_diag_ready = sem("v_diag_ready")
        v_spread = sem("v_spread")
        v_rows_ready = sem("v_rows_ready")
        w_summed = sem("w_summed")
        sum_loaded = [sem(f"sum_loaded{k}") for k in range(2)]
        adj_summed = sem("adj_summed")
        peak_ready = sem("peak_ready")
        peaks_ready = sem("peaks_ready")
        scale_step = sem("scale_step")
        w_hi_ready = sem("w_hi_ready")
        w_split = sem("w_split")
        adj_hi_ready = sem("adj_hi_ready")
        adj_lo_ready = sem("adj_lo_ready")
        low_summed = sem("low_summed")
        adj_turned = [sem(f"adj_turned{k}") for k in range(4)]
        inexact_ready = sem("inexact_ready")

        x_loaded = [sem(f"x_loaded{k}") for k in range(4)]
        adj_loaded = [sem(f"adj_loaded{k}") for k in range(2)]
        x_reloaded = [sem(f"x_reloaded{k}") for k in range(T)]
        stored = [sem(f"stored{k}") for k in range(T)]
        stats0_taken = sem("stats0_taken")
        mean0_ready = sem("mean0_ready")
        var0_ready = sem("var0_ready")
        rstd0_ready = sem("rstd0_ready")
        shift0_ready = sem("shift0_ready")
        h0_ready = sem("h0_ready")
        h0_hi_ready = sem("h0_hi_ready")
        h0_lo_ready = sem("h0_lo_ready")
        s1_ready = sem("s1_ready")
        s2_ready = sem("s2_ready")
        s2_diag_ready = sem("s2_diag_ready")
        s2_spread = sem("s2_spread")
        scores_ready = sem("scores_ready")
        leaky_ready = sem("leaky_ready")
        masked_ready = sem("masked_ready")
        minus_top_ready = sem("minus_top_ready")
        exp_ready = sem("exp_ready")
        beta_denom_ready = sem("beta_denom_ready")
        diag_added = sem("diag_added")
        inv_denom_ready = sem("inv_denom_ready")
        z_rows_ready = sem("z_rows_ready")
        rows_hi_ready = sem("rows_hi_ready")
        rows_lo_ready = sem("rows_lo_ready")
        rows_turned = [sem(f"rows_turned{k}") for k in range(2)]
        att_done = sem("att_done")
        gT_hi_ready = sem("gT_hi_ready")
        gT_lo_ready = sem("gT_lo_ready")
        gw_done = sem("gw_done")
        elu_exp_ready = sem("elu_exp_ready")
        elu_low_ready = sem("elu_low_ready")
        elu_ready = sem("elu_ready")
        x1_ready = sem("x1_ready")
        stats1_taken = sem("stats1_taken")
        mean1_ready = sem("mean1_ready")
        var1_ready = sem("var1_ready")
        rstd1_ready = sem("rstd1_ready")
        shift1_ready = sem("shift1_ready")
        h1_ready = sem("h1_ready")
        h1_hi_ready = sem("h1_hi_ready")
        h1_lo_ready = sem("h1_lo_ready")
        x1_bias_ready = sem("x1_bias_ready")
        y_done = sem("y_done")
        yT_hi_ready = sem("yT_hi_ready")
        yT_lo_ready = sem("yT_lo_ready")
        out_done = sem("out_done")
        result_ready = sem("result_ready")

        emptied = {"att": gT_lo_ready, "y": yT_lo_ready, "out": result_ready, "gw": elu_ready}

        def wait_apart(eng, *waits):
            waits = [(sem, value if isinstance(value, int) else eng.to_reg(value)) for sem, value in waits]
            eng.wait_ge(consts_ready, 4)
            for sem, value in waits:
                at_least(eng, sem, value)

        block = ctx.enter_context(nc.Block())

        @block.sync
        def _(sp):
            for k in range(2):
                sp.dma_start(a_rows[:, k, :], a[k * C:(k + 1) * C, 0].partition_broadcast(P)).then_inc(a_loaded, 16)
            for k in range(K):
                sp.dma_start(x1[:, k, :], W[k * P:(k + 1) * P, :]).then_inc(w_loaded[k], 16)
            sp.dma_start(betas[:, :], beta.partition_broadcast(P)).then_inc(beta_loaded, 16)

            def tile_of(tensor, b, n):
                return tensor[bass.ds(b.number, 1), n * P:(n + 1) * P, :].rearrange("o p c -> (o p) c")

            def step(b, time):
                for n in tiles_at(OUT, time):
                    sp.wait_ge(result_ready, b.count(T, n + 1))
                    sp.dma_start(tile_of(out, b, n), x1[:, n, :]).then_inc(stored[n], 16)
                for n in tiles_at(RELOAD_X, time):
                    at_least(sp, stored[n], b.count(16, 0))
                    if b.first:
                        sp.wait_ge(w_split, 1 + n // K)
                    sp.dma_start(x1[:, n, :], tile_of(x, b, n)).then_inc(x_reloaded[n], 16)
                for n in tiles_at([t + 5 for t in PRE], time):
                    wait_apart(sp, (rows_lo_ready, b.count(T, n + 1)),
                                   (att_done, b.count(T, TH * (n // TH + 1) - T)))
                    for rows, turned in ((rows_hi, PT_hi), (rows_lo, PT_lo)):
                        sp.dma_start_transpose(turned[:, :, n * P:(n + 1) * P], rows[:, n % 2, :])\
                            .then_inc(rows_turned[n % 2], 16)
                for n in tiles_at(LOAD_X, time):
                    at_least(sp, h0_ready, b.count(T, n + 1 - 4))
                    sp.dma_start(x_in[:, n % 4, :], tile_of(x, b, n)).then_inc(x_loaded[n % 4], 16)
                for n in tiles_at(LOAD_ADJ, time):
                    at_least(sp, masked_ready, b.count(T, n + 1 - 2))
                    if b.first and n == 0:
                        sp.wait_ge(adj_summed, T)
                    elif b.first and n >= 2:
                        sp.wait_ge(adj_lo_ready, n + 1 - 2)
                    elif b.second and n < 2:
                        sp.wait_ge(adj_lo_ready, T + n + 1 - 2)
                    sp.dma_start(adj_in[:, n % 2, :], adj[n * P:(n + 1) * P, :]).then_inc(adj_loaded[n % 2], 16)

            def setup(time):
                for n in tiles_at(SUM_ADJ, time):
                    if n >= 2:
                        sp.wait_ge(adj_summed, n + 1 - 2)
                    sp.dma_start(adj_in[:, n % 2, :], adj[n * P:(n + 1) * P, :]).then_inc(sum_loaded[n % 2], 16)
                if time == SUM_W[1] - 3:
                    sp.dma_start(w2_in.rearrange("p (k c) -> p k c", k=K), weight.rearrange("(k p) c -> p k c", p=P))\
                        .then_inc(w2_loaded, 16)
                if time == SUM_W[1]:
                    sp.dma_start(bias_rows[:, :], bias.partition_broadcast(P)).then_inc(bias_loaded, 16)
                for n in tiles_at([t + 2 for t in PARTS], time):
                    sp.wait_ge(adj_lo_ready, n + 1)
                    for rows, turned in ((adj_rows_hi, adjT_hi), (adj_rows_lo, adjT_lo)):
                        sp.dma_start_transpose(turned[:, :, n * P:(n + 1) * P], rows[:, n % 4, :])\
                            .then_inc(adj_turned[n % 4], 16)

            def iteration(batches, _):
                for slot in range(SLOTS):
                    for stage in sorted(batches, reverse=True):
                        step(batches[stage], SLOTS * stage + slot)
                        if batches[stage].first:
                            setup(SLOTS * stage + slot)

            run(sp, iteration)
            for n in range(T):
                sp.wait_ge(stored[n], 16 * B)

        @block.gpsimd
        def _(pool):
            pool.memset(ident[:, :], 0.0).then_inc(consts_ready, 1)
            pool.memset(ones[:, :], 1.0).then_inc(consts_ready, 1)
            pool.memset(minus_half[:, :], -0.5).then_inc(consts_ready, 1)
            pool.wait_ge(consts_ready, 1)
            pool.affine_select(out=ident[:, :], in_=ident[:, :], compare_op=ALU.not_equal, fill=1.0, base=0,
                               pattern=[[-1, P]], channel_multiplier=1).then_inc(consts_ready, 1)
            pool.wait_ge(consts_ready, 4)
            for k in range(2 * K):
                pool.wait_ge(v_cols_ready, k + 1)
                pool.tensor_scalar(v_diag[:, k, :], ident[:, :], v_cols[:, k:k + 1], None, ALU.mult)\
                    .then_inc(v_diag_ready, 1)
            pool.wait_ge(beta_loaded, 16)

            def norm_scale(b, n, mean_sem, mean, var_sem, var, rstd_sem, rstd, shift_sem, shift):
                wait_apart(pool, (mean_sem, b.count(T, n + 1)))
                pool.tensor_scalar(var[:, n:n + 1], mean[:, n, 1:2], H_SCALE ** -2, EPS * H_SCALE ** -2,
                                   ALU.mult, ALU.add).then_inc(var_sem, 1)
                pool.wait_ge(var_sem, b.count(T, n + 1))
                pool.tensor_tensor(rstd[:, n:n + 1], var[:, n:n + 1], minus_half[:, :], ALU.pow).then_inc(rstd_sem, 1)
                wait_apart(pool, (rstd_sem, b.count(T, n + 1)))
                pool.tensor_scalar(shift[:, n:n + 1], mean[:, n, 0:1], rstd[:, n:n + 1], -1.0,
                                   ALU.mult, ALU.mult).then_inc(shift_sem, 1)

            def step(b, time):
                for n in tiles_at([t + 1 for t in GW], time):
                    norm_scale(b, n, mean1_ready, mean1, var1_ready, var1, rstd1_ready, rstd1, shift1_ready, shift1)
                for n in tiles_at([t + 1 for t in PRE], time):
                    wait_apart(pool, (masked_ready, b.count(T, n + 1)))
                    pool.tensor_scalar(minus_top[:, n:n + 1], top[:, n:n + 1], -1.0, None, ALU.mult)\
                        .then_inc(minus_top_ready, 1)
                for n in tiles_at([t + 2 for t in PRE], time):
                    wait_apart(pool, (exp_ready, b.count(T, n + 1)),
                                     (diag_added, b.count(T, n + 1 - T)))
                    pool.tensor_scalar(beta_denom[:, n:n + 1], denom[:, b.parity, n:n + 1], betas[:, 0:1], None, ALU.mult)\
                        .then_inc(beta_denom_ready, 1)
                for n in tiles_at(NORM0, time):
                    norm_scale(b, n, mean0_ready, mean0, var0_ready, var0, rstd0_ready, rstd0, shift0_ready, shift0)
                for n in tiles_at([t - 1 for t in SPREAD], time):
                    wait_apart(pool, (s2_ready, b.count(T, n + 1)),
                                     (s2_spread, b.count(T, n + 1 - 2)))
                    pool.tensor_scalar(s2_diag[:, n % 2, :], ident[:, :], s2[:, n:n + 1], None, ALU.mult)\
                        .then_inc(s2_diag_ready, 1)
                for n in tiles_at([t + 3 for t in GW], time):
                    pool.wait_ge(h1_hi_ready, b.count(T, n + 1))
                    pool.tensor_tensor(h1_lo[:, n, :], h1[:, n % 2, :], h1_hi[:, n, :], ALU.subtract)\
                        .then_inc(h1_lo_ready, 1)
                for n in tiles_at([t + 8 for t in GW], time):
                    pool.tensor_tensor(x1[:, n, :], x1[:, n, :], bias_rows[:, :], ALU.add).then_inc(x1_bias_ready, 1)
                for n in tiles_at([t + 1 for t in H0], time):
                    pool.wait_ge(h0_hi_ready, b.count(T, n + 1))
                    at_least(pool, att_done, b.count(T, -T))
                    pool.tensor_tensor(h0_lo[:, b.parity, n, :], h0[:, n % 2, :], h0_hi[:, b.parity, n, :], ALU.subtract)\
                        .then_inc(h0_lo_ready, 1)

            def group(b, time):
                for n in tiles_at(GW, time):
                    pool.wait_ge(elu_ready, b.count(T, n + 1))
                    pool.wait_ge(x_reloaded[n], b.count(16, 16))
                    pool.tensor_tensor(x1[:, n, :], x1[:, n, :], elu[:, n % 2, :], ALU.add).then_inc(x1_ready, 1)

            def setup(time):
                if time == SCALES - 1:
                    pool.wait_ge(w_summed, 2)
                    pool.wait_ge(peak_ready, 1)
                    pool.partition_all_reduce(peaks[:, 0:3], peak[:, 0:3], P, ABSMAX).then_inc(peaks_ready, 1)
                    pool.wait_ge(bias_loaded, 16)
                if time == INEXACT:
                    pool.wait_ge(peak_ready, 2)
                    pool.partition_all_reduce(peaks[:, 3:4], peak[:, 3:4], P, ABSMAX).then_inc(peaks_ready, 1)

            def iteration(batches, _):
                for slot in range(SLOTS):
                    for stage in sorted(batches, reverse=True):
                        step(batches[stage], SLOTS * stage + slot)
                        if batches[stage].first:
                            setup(SLOTS * stage + slot)
                    for stage in batches:
                        group(batches[stage], SLOTS * stage + slot)

            run(pool, iteration)

        @block.scalar
        def _(act):

            def setup(time):
                for n in tiles_at(SUM_ADJ, time):
                    act.wait_ge(sum_loaded[n % 2], 16 * (n // 2 + 1))
                    act.activation(adj_in[:, n % 2, :], adj_in[:, n % 2, :], ACT.Abs, accum_out=adj_sums[:, n:n + 1])\
                        .then_inc(adj_summed, 1)
                for k in tiles_at(SUM_W, time):
                    for loaded in (w_loaded, [w2_loaded])[k]:
                        act.wait_ge(loaded, 16)
                    if k == 1:
                        act.wait_ge(w_summed, 1)
                    act.activation(abs_w, (W_in, w2_in)[k], ACT.Abs, accum_out=peak[:, k:k + 1]).then_inc(w_summed, 1)
                if time == H0[0]:
                    act.wait_ge(v_spread, 1)
                    act.activation(v_rows[:, :, :].rearrange("p k c -> p (k c)"), s2_rows[0][:, :], ACT.Copy).then_inc(v_rows_ready, 1)
                if time == SCALES:
                    act.wait_ge(scale_step, 13)
                for k in tiles_at(SPLIT, time):
                    act.activation((w_hi, w2_hi)[k][:, :, :].rearrange("p k c -> p (k c)"), (W_in, w2_in)[k], ACT.Copy,
                                   scale=(w_scale, w2_scale)[k]).then_inc(w_hi_ready, 1)
                for n in tiles_at(PARTS, time):
                    act.wait_ge(adj_loaded[n % 2], 16 * (n // 2 + 1))
                    if n >= 4:
                        act.wait_ge(adj_turned[n % 4], 32)
                    act.activation(adj_rows_hi[:, n % 4, :], adj_in[:, n % 2, :], ACT.Copy, scale=adj_scale)\
                        .then_inc(adj_hi_ready, 1)
                for n in tiles_at([t + 3 for t in PARTS], time):
                    act.wait_ge(adj_lo_ready, n + 1)
                    if n >= 4:
                        act.wait_ge(low_summed, n + 1 - 4)
                    act.activation(abs_low[:, n % 4, :], adj_rows_lo[:, n % 4, :], ACT.Abs, accum_out=low_sums[:, n:n + 1])\
                        .then_inc(low_summed, 1)

            def step(b, time):
                for n in tiles_at([t + 4 for t in PRE], time):
                    act.wait_ge(diag_added, b.count(T, n + 1))
                    at_least(act, rows_turned[n % 2], b.count(128, 32 * (n // 2)))
                    act.activation(rows_hi[:, n % 2, :], probs[:, n % 2, :], ACT.Copy, scale=p_scale)\
                        .then_inc(rows_hi_ready, 1)
                for n in tiles_at([t + 2 for t in PRE], time):
                    act.wait_ge(minus_top_ready, b.count(T, n + 1))
                    act.activation(probs[:, n % 2, :], probs[:, n % 2, :], ACT.Exp, bias=minus_top[:, n:n + 1],
                                   accum_out=denom[:, b.parity, n:n + 1]).then_inc(exp_ready, 1)
                for n in tiles_at([t + 3 for t in GW], time):
                    act.wait_ge(h1_ready, b.count(T, n + 1))
                    act.activation(h1_hi[:, n, :], h1[:, n % 2, :], ACT.Copy).then_inc(h1_hi_ready, 1)
                for n in tiles_at([t + 2 for t in GW], time):
                    act.wait_ge(shift1_ready, b.count(T, n + 1))
                    at_least(act, h1_lo_ready, b.count(T, n + 1 - 2))
                    act.activation(h1[:, n % 2, :], x1[:, n, :], ACT.Relu, bias=shift1[:, n:n + 1],
                                   scale=rstd1[:, n:n + 1]).then_inc(h1_ready, 1)
                for n in tiles_at([t + 1 for t in H0], time):
                    act.wait_ge(h0_ready, b.count(T, n + 1))
                    at_least(act, att_done, b.count(T, -T))
                    act.activation(h0_hi[:, b.parity, n, :], h0[:, n % 2, :], ACT.Copy).then_inc(h0_hi_ready, 1)
                for n in tiles_at(H0, time):
                    act.wait_ge(shift0_ready, b.count(T, n + 1))
                    at_least(act, h0_lo_ready, b.count(T, n + 1 - 2))
                    at_least(act, s2_ready, b.count(T, n + 1 - 2))
                    act.activation(h0[:, n % 2, :], x_in[:, n % 4, :], ACT.Relu, bias=shift0[:, n:n + 1],
                                   scale=rstd0[:, n:n + 1]).then_inc(h0_ready, 1)
                for n in tiles_at(PRE, time):
                    act.wait_ge(s2_spread, b.count(T, T))
                    at_least(act, rows_lo_ready, b.count(T, n + 1 - 2))
                    if b.first and n == 0:
                        act.wait_ge(w_summed, 2)
                    act.activation(probs[:, n % 2, :], s2_rows[b.parity][:, :], ACT.Identity, bias=s1[:, b.parity, n:n + 1])\
                        .then_inc(scores_ready, 1)

            def group(b, time):
                for n in tiles_at(ATT, time):
                    half, c = divmod(n, K)
                    act.wait_ge(att_done, b.count(T, n + 1))
                    act.activation(gT_hi[:, c, :], sums[c][:, :], ACT.Copy, scale=g_scale).then_inc(gT_hi_ready, 1)
                for n in tiles_at(GW, time):
                    act.wait_ge(gw_done, b.count(T, n + 1))
                    act.wait_ge(z_rows_ready, b.count(1, 1))
                    at_least(act, x1_ready, b.count(T, n + 1 - 2))
                    act.activation(elu[:, n % 2, :], sums[n % 4][:, :], ACT.Exp, scale=z_rows[:, b.parity, n:n + 1])\
                        .then_inc(elu_exp_ready, 1)
                for n in tiles_at(Y, time):
                    half, d = divmod(n, K)
                    act.wait_ge(y_done, b.count(T, n + 1))
                    act.activation(yT_hi[:, d, half * HALF:(half + 1) * HALF], sums[d][:, :], ACT.Copy,
                                   scale=Y_SCALE / (TOP * H_SCALE)).then_inc(yT_hi_ready, 1)

            def iteration(batches, _):
                for slot in range(SLOTS):
                    for stage in sorted(batches, reverse=True):
                        step(batches[stage], SLOTS * stage + slot)
                        if batches[stage].first:
                            setup(SLOTS * stage + slot)
                    for stage in batches:
                        group(batches[stage], SLOTS * stage + slot)

            run(act, iteration)

        @block.vector
        def _(dve):
            dve.wait_ge(a_loaded, 32)
            for k in range(2 * K):
                dve.wait_ge(w_loaded[k % K], 16)
                if k >= 1:
                    dve.wait_ge(v_cols_ready, k)
                dve.tensor_tensor_reduce(junk[:, :], W_in[:, (k % K) * C:(k % K + 1) * C], a_rows[:, k // K, :],
                                         1.0 / H_SCALE, 0.0, ALU.mult, ALU.add, v_cols[:, k:k + 1]).then_inc(v_cols_ready, 1)

            def scales():
                dve.wait_ge(beta_loaded, 16)
                dve.scalar_tensor_tensor(bound[:, 4:5], betas[:, :], -1.0, betas[:, :], ALU.mult, ALU.max).then_inc(scale_step, 1)
                dve.wait_ge(scale_step, 1)
                dve.tensor_scalar(bound[:, 3:4], bound[:, 4:5], float(N), 1.0, ALU.mult, ALU.add).then_inc(scale_step, 1)
                dve.wait_ge(scale_step, 2)
                dve.tensor_scalar(bound[:, 4:5], bound[:, 4:5], 1.0, None, ALU.add).then_inc(scale_step, 1)
                dve.wait_ge(peaks_ready, 1)
                dve.tensor_scalar(bound[:, 0:3], peaks[:, 0:3], TINY, None, ALU.max).then_inc(scale_step, 1)
                dve.wait_ge(scale_step, 4)
                dve.tensor_scalar(pow2[:, :].bitcast(I32), bound[:, :].bitcast(I32), EXPONENT, None, ALU.bitwise_and)\
                    .then_inc(scale_step, 1)
                dve.wait_ge(scale_step, 5)
                dve.reciprocal(inv2[:, :], pow2[:, :]).then_inc(scale_step, 1)
                dve.wait_ge(scale_step, 6)
                dve.tensor_scalar(scale[:, 0:4], inv2[:, 0:4], TOP, None, ALU.mult).then_inc(scale_step, 1)
                dve.tensor_scalar(bound[:, 0:1], pow2[:, 3:4], 1.0 / (H_SCALE * TOP), None, ALU.mult).then_inc(scale_step, 1)
                dve.tensor_scalar(bound[:, 1:2], pow2[:, 4:5], 1.0 / TOP, None, ALU.mult).then_inc(scale_step, 1)
                dve.tensor_scalar(bound[:, 2:3], pow2[:, 2:3], 1.0 / (TOP * Y_SCALE), None, ALU.mult).then_inc(scale_step, 1)
                dve.wait_ge(scale_step, 10)
                dve.tensor_tensor(g_scale, bound[:, 0:1], inv2[:, 4:5], ALU.mult).then_inc(scale_step, 1)
                dve.tensor_tensor(z_scale, bound[:, 1:2], pow2[:, 0:1], ALU.mult).then_inc(scale_step, 1)
                dve.tensor_tensor(o_scale, bound[:, 2:3], pow2[:, 1:2], ALU.mult).then_inc(scale_step, 1)
                dve.wait_ge(scale_step, 13)

            def setup(time):
                if time == H0[0]:
                    dve.wait_ge(v_rows_ready, 1)
                if time == SCALES - 2:
                    dve.wait_ge(adj_summed, T)
                    dve.tensor_reduce(peak[:, 2:3], adj_sums[:, :], AX.X, ALU.max).then_inc(peak_ready, 1)
                if time == SCALES:
                    scales()
                for k in tiles_at(SPLIT, time):
                    hi, lo = ((w_hi, w_lo), (w2_hi, w2_lo))[k]
                    dve.wait_ge(w_hi_ready, k + 1)
                    dve.scalar_tensor_tensor(lo[:, :, :].rearrange("p k c -> p (k c)"), (W_in, w2_in)[k], (w_scale, w2_scale)[k],
                                             hi[:, :, :].rearrange("p k c -> p (k c)"), ALU.mult, ALU.subtract).then_inc(w_split, 1)
                for n in tiles_at([t + 1 for t in PARTS], time):
                    dve.wait_ge(adj_hi_ready, n + 1)
                    if n >= 4:
                        dve.wait_ge(low_summed, n + 1 - 4)
                    dve.scalar_tensor_tensor(adj_rows_lo[:, n % 4, :], adj_in[:, n % 2, :], adj_scale, adj_rows_hi[:, n % 4, :],
                                             ALU.mult, ALU.subtract).then_inc(adj_lo_ready, 1)
                if time == INEXACT:
                    dve.wait_ge(low_summed, T)
                    dve.tensor_reduce(peak[:, 3:4], low_sums[:, :], AX.X, ALU.max).then_inc(peak_ready, 1)
                    dve.wait_ge(peaks_ready, 2)
                    dve.tensor_scalar(inexact[:, :], peaks[:, 3:4], 0.0, None, ALU.is_gt).then_inc(inexact_ready, 1)

            def step(b, time):
                for n in tiles_at([t + 4 for t in PRE], time):
                    dve.wait_ge(rows_hi_ready, b.count(T, n + 1))
                    dve.scalar_tensor_tensor(rows_lo[:, n % 2, :], probs[:, n % 2, :], p_scale, rows_hi[:, n % 2, :],
                                             ALU.mult, ALU.subtract).then_inc(rows_lo_ready, 1)
                for n in tiles_at([t + 3 for t in PRE], time):
                    own = probs[:, n % 2, n * P:(n + 1) * P]
                    dve.wait_ge(beta_denom_ready, b.count(T, n + 1))
                    dve.scalar_tensor_tensor(own, ident[:, :], beta_denom[:, n:n + 1], own, ALU.mult, ALU.add)\
                        .then_inc(diag_added, 1)
                if time == RECIP:
                    dve.wait_ge(exp_ready, b.count(T, T))
                    at_least(dve, z_rows_ready, b.count(1, 0))
                    dve.reciprocal(inv_denom[:, :], denom[:, b.parity, :]).then_inc(inv_denom_ready, 1)
                    dve.wait_ge(inv_denom_ready, b.count(1, 1))
                    dve.tensor_scalar(z_rows[:, b.parity, :], inv_denom[:, :], z_scale, None, ALU.mult).then_inc(z_rows_ready, 1)
                for n in tiles_at([t + 1 for t in GW], time):
                    dve.wait_ge(x1_ready, b.count(T, n + 1))
                    dve.bn_stats(stats1[:, n, :], x1[:, n, :]).then_inc(stats1_taken, 1)
                    wait_apart(dve, (stats1_taken, b.count(T, n + 1)))
                    dve.bn_aggr(mean1[:, n, :], stats1[:, n, :]).then_inc(mean1_ready, 1)
                for n in tiles_at([t + 1 for t in PRE], time):
                    own = probs[:, n % 2, :]
                    dve.wait_ge(scores_ready, b.count(T, n + 1))
                    dve.scalar_tensor_tensor(own, own, SLOPE, own, ALU.mult, ALU.max).then_inc(leaky_ready, 1)
                    wait_apart(dve, (leaky_ready, b.count(T, n + 1)),
                                    (adj_loaded[n % 2], b.count(64, 16 * (n // 2 + 1))))
                    dve.tensor_tensor_reduce(own, own, adj_in[:, n % 2, :], 1.0, -HUGE, ALU.mult, ALU.max, top[:, n:n + 1])\
                        .then_inc(masked_ready, 1)
                for n in tiles_at([t + 1 for t in H0], time):
                    dve.wait_ge(h0_ready, b.count(T, n + 1))
                    at_least(dve, s2_ready, b.count(T, n))
                    dve.tensor_tensor_reduce(junk[:, :], h0[:, n % 2, :], v_rows[:, 0, :], 1.0, 0.0, ALU.mult, ALU.add,
                                             s1[:, b.parity, n:n + 1]).then_inc(s1_ready, 1)
                    dve.wait_ge(s1_ready, b.count(T, n + 1))
                    dve.tensor_tensor_reduce(junk[:, :], h0[:, n % 2, :], v_rows[:, 1, :], 1.0, 0.0, ALU.mult, ALU.add,
                                             s2[:, n:n + 1]).then_inc(s2_ready, 1)
                for n in tiles_at(NORM0, time):
                    dve.wait_ge(x_loaded[n % 4], b.count(32, 16 * (n // 4 + 1)))
                    dve.bn_stats(stats0[:, n, :], x_in[:, n % 4, :]).then_inc(stats0_taken, 1)
                    wait_apart(dve, (stats0_taken, b.count(T, n + 1)))
                    dve.bn_aggr(mean0[:, n, :], stats0[:, n, :]).then_inc(mean0_ready, 1)

            def group(b, time):
                for n in tiles_at(ATT, time):
                    c = n % K
                    dve.wait_ge(gT_hi_ready, b.count(T, n + 1))
                    dve.scalar_tensor_tensor(gT_lo[:, c, :], sums[c][:, :], g_scale, gT_hi[:, c, :], ALU.mult, ALU.subtract)\
                        .then_inc(gT_lo_ready, 1)
                for n in tiles_at(GW, time):
                    own = elu[:, n % 2, :]
                    dve.wait_ge(elu_exp_ready, b.count(T, n + 1))
                    dve.tensor_scalar(own, own, 1.0, -1.0, ALU.min, ALU.add).then_inc(elu_low_ready, 1)
                    dve.wait_ge(elu_low_ready, b.count(T, n + 1))
                    dve.scalar_tensor_tensor(own, sums[n % 4][:, :], z_rows[:, b.parity, n:n + 1], own, ALU.mult, ALU.max)\
                        .then_inc(elu_ready, 1)
                for n in tiles_at(Y, time):
                    half, d = divmod(n, K)
                    dve.wait_ge(yT_hi_ready, b.count(T, n + 1))
                    dve.scalar_tensor_tensor(yT_lo[:, d, half * HALF:(half + 1) * HALF], sums[d][:, :], Y_SCALE / (TOP * H_SCALE),
                                             yT_hi[:, d, half * HALF:(half + 1) * HALF], ALU.mult, ALU.subtract)\
                        .then_inc(yT_lo_ready, 1)
                for n in tiles_at(OUT, time):
                    dve.wait_ge(out_done, b.count(T, n + 1))
                    dve.wait_ge(x1_bias_ready, b.count(T, n + 1))
                    dve.scalar_tensor_tensor(x1[:, n, :], sums[n % 4][:, :], o_scale, x1[:, n, :], ALU.mult, ALU.add)\
                        .then_inc(result_ready, 1)

            def iteration(batches, _):
                for slot in range(SLOTS):
                    for stage in sorted(batches, reverse=True):
                        step(batches[stage], SLOTS * stage + slot)
                        if batches[stage].first:
                            setup(SLOTS * stage + slot)
                    for stage in batches:
                        group(batches[stage], SLOTS * stage + slot)

            run(dve, iteration)

        @block.tensor
        def _(pe):
            def spread(into, k, diag):
                return pe.matmul(into[:, k * P:(k + 1) * P], ones[:, :], diag, start=True, stop=True)

            pe.wait_ge(consts_ready, 4)
            for k in range(2 * K):
                pe.wait_ge(v_diag_ready, k + 1)
                last = spread(s2_rows[0], k, v_diag[:, k, :])
            last.then_inc(v_spread, 1)
            low = []

            def before_loop():
                pe.wait_ge(w_split, 2)
                for turned in adj_turned:
                    pe.wait_ge(turned, 64)
                pe.wait_ge(inexact_ready, 1)
                low.append(pe.value_load(inexact[0:1, 0:1], min_val=0, max_val=1))

            def bank_free(k, i, batches, last_batches):
                for back in range(1, len(BLOCKS)):
                    kind, half, stage = BLOCKS[k - back]
                    present = batches if back <= k else last_batches
                    if stage in present:
                        at_least(pe, emptied[kind], present[stage].count(T, TH * half + i + 1))
                        return

            def products(bank, pairs):
                for j, (stationary, moving) in enumerate(pairs):
                    last = pe.matmul(bank, stationary, moving, start=(j == 0), stop=(j == len(pairs) - 1))
                return last

            def group(b, time, batches, last_batches):
                bank_free((time % SLOTS) // TH, time % TH, batches, last_batches)
                for n in tiles_at(ATT, time):
                    half, c = divmod(n, K)
                    cols, rows = slice(c * P, (c + 1) * P), slice(half * HALF, (half + 1) * HALF)
                    if c == 0:
                        for turned in rows_turned:
                            pe.wait_ge(turned, b.count(128, 64 * (half + 1)))
                        pe.wait_ge(h0_lo_ready, b.count(T, T))
                    products(sums[c][:, :], [
                        pair for j in range(T) for pair in (
                            (h0_hi[:, b.parity, j, cols], PT_hi[:, j, rows]),
                            (h0_hi[:, b.parity, j, cols], PT_lo[:, j, rows]),
                            (h0_lo[:, b.parity, j, cols], PT_hi[:, j, rows]))
                    ]).then_inc(att_done, 1)
                for n in tiles_at(GW, time):
                    rows = slice((n % TH) * P, (n % TH + 1) * P)
                    if b.first and n == 0:
                        pe.wait_ge(w_split, 1)
                    pe.wait_ge(gT_lo_ready, b.count(T, TH * (n // TH + 1)))
                    products(sums[n % 4][:, :], [
                        pair for c in range(K) for pair in (
                            (gT_hi[:, c, rows], w_hi[:, c, :]),
                            (gT_hi[:, c, rows], w_lo[:, c, :]),
                            (gT_lo[:, c, rows], w_hi[:, c, :]))
                    ]).then_inc(gw_done, 1)
                for n in tiles_at(Y, time):
                    half, d = divmod(n, K)
                    cols, rows = slice(d * P, (d + 1) * P), slice(half * HALF, (half + 1) * HALF)
                    if n == 0:
                        pe.wait_ge(h1_lo_ready, b.count(T, T))
                    bank = sums[d][:, :]
                    pe.matmul(bank, h1_hi[:, 0, cols], adjT_hi[:, 0, rows], start=True, stop=False)
                    with pe.If(low[0] > 0):
                        for j in range(T):
                            pe.matmul(bank, h1_hi[:, j, cols], adjT_lo[:, j, rows], start=False, stop=False)
                    for j in range(1, T):
                        pe.matmul(bank, h1_hi[:, j, cols], adjT_hi[:, j, rows], start=False, stop=False)
                    for j in range(T):
                        last = pe.matmul(bank, h1_lo[:, j, cols], adjT_hi[:, j, rows], start=False, stop=(j == T - 1))
                    last.then_inc(y_done, 1)
                for n in tiles_at(OUT, time):
                    rows = slice(n * P, (n + 1) * P)
                    pe.wait_ge(yT_lo_ready, b.count(T, TH * (n // TH + 1)))
                    products(sums[n % 4][:, :], [
                        pair for d in range(K) for pair in (
                            (yT_hi[:, d, rows], w2_hi[:, d, :]),
                            (yT_hi[:, d, rows], w2_lo[:, d, :]),
                            (yT_lo[:, d, rows], w2_hi[:, d, :]))
                    ]).then_inc(out_done, 1)

            def step(b, time):
                for n in tiles_at(SPREAD, time):
                    pe.wait_ge(s2_diag_ready, b.count(T, n + 1))
                    if n == 0:
                        at_least(pe, scores_ready, b.count(T, -T))
                        if b.first:
                            pe.wait_ge(v_rows_ready, 1)
                    spread(s2_rows[b.parity], n, s2_diag[:, n % 2, :]).then_inc(s2_spread, 1)

            def iteration(batches, last_batches):
                for slot in range(SLOTS):
                    for stage in batches:
                        time = SLOTS * stage + slot
                        if time in ATT + GW + Y + OUT:
                            group(batches[stage], time, batches, last_batches)
                    for stage in sorted(batches, reverse=True):
                        step(batches[stage], SLOTS * stage + slot)

            run(pe, iteration, before_loop)


_INS = ["x", "adj", "L0_gnn_W", "L0_gnn_a", "L0_gnn_beta", "L1_gnn_weight", "L1_gnn_bias"]
_OUTS = [((16, 1024, 512), "float32")]


def kernel(**inputs):
    import numpy as _np
    import concourse.bacc as _bacc
    from concourse import mybir as _mybir
    from concourse.bass_utils import run_bass_kernel_spmd as _run

    nc = _bacc.Bacc("TRN2", target_bir_lowering=False, num_devices=1, dynamic_dma_scratch_size=1024)
    arrays, args = {}, []
    for name in _INS:
        a = _np.ascontiguousarray(inputs[name])
        arrays[f"in_{name}_dram"] = a
        args.append(nc.dram_tensor(f"in_{name}_dram", a.shape, _mybir.dt.from_np(a.dtype), kind="ExternalInput").ap())
    for i, (shape, dtype) in enumerate(_OUTS):
        dt = _mybir.dt.from_np(_np.dtype(dtype))
        args.append(nc.dram_tensor(f"out_{i}_dram", shape, dt, kind="ExternalOutput").ap())
    two_layers(nc, *args)
    r = _run(nc, [arrays], core_ids=[0])
    return r.results[0]["out_0_dram"]
```

```python
from contextlib import ExitStack

import concourse.bass as bass
from concourse import mybir

F32 = mybir.dt.float32
F16 = mybir.dt.float16
I32 = mybir.dt.int32
ALU = mybir.AluOpType
ACT = mybir.ActivationFunctionType
AX = mybir.AxisListType
ABSMAX = bass.bass_isa.ReduceOp.absmax

P = 128
SLOTS = 32
STAGES = 3
EPS = 1e-5
SLOPE = 0.2
HUGE = 3.0e38
TINY = 1.0e-30
SCALE_STEPS = 12
EXPONENT = 0x7F800000
H_SCALE = 2.0 ** 11
TOP = 2.0 ** 14
Y_SCALE = 2.0 ** 10

NORM0 = [0, 0, 1, 1, 4, 6, 8, 10]
H0 = [1, 2, 4, 5, 7, 9, 11, 12]
SPREAD = [4, 8, 8, 9, 12, 13, 16, 17]
PRE = [18, 19, 22, 24, 34, 36, 38, 41]
RECIP = PRE[7] + 4
ATT = [32, 33, 34, 35, 52, 53, 54, 55]
GW = [48, 49, 50, 51, 60, 61, 62, 63]
Y = [68, 69, 70, 71, 72, 73, 74, 75]
OUT = [76, 77, 78, 79, 88, 89, 90, 91]
SUM_W = [14, 14]
SCALES = 18
SPLIT = [31, 38]
SUM_ADJ = [22, 23, 25, 27, 38, 39, 39, 39]
SCALE_ADJ = [28, 40]
PARTS = [30, 31, 31, 33, 42, 42, 43, 44]
INEXACT = 46
LOAD_W2 = 4
LOAD_STAGE = [5, 5, 6, 6] + [t + 3 for t in PARTS[:4]]
PRE_FIRST = [18, 20, 22, 24, 26, 28, 31, 32]
PRE_SECOND = [4, 6, 8, 10] + PRE[4:]
LEAD = 16
ATT_FIRST = [32, 35, 36, 37, 46, 47, 48, 49]
GW_FIRST = [40, 41, 42, 43, 56, 57, 58, 59]
RECIP_FIRST = PRE_FIRST[7] + 4
RELOAD_X_FIRST = [t - 3 for t in GW_FIRST]
LOAD_X = [0, 0, 0, 0] + [t + 1 for t in H0[:4]]
LOAD_ADJ = [8, 11]
LOAD_ADJ_SECOND = [0, 2]
RELOAD_X = [t - SLOTS + 1 for t in OUT]
BLOCKS = [("att", 0, 1), ("y", 0, 2), ("y", 1, 2), ("out", 0, 2), ("gw", 0, 1), ("att", 1, 1), ("out", 1, 2), ("gw", 1, 1)]


def led(b, times):
    return [t - LEAD for t in times] if b.second else times


def pre(b):
    return PRE_FIRST if b.first else PRE_SECOND if b.second else PRE


def att(b):
    return ATT_FIRST if b.first else ATT


def gw(b):
    return GW_FIRST if b.first else GW


def load_adj(b):
    return (LOAD_ADJ_SECOND if b.second else LOAD_ADJ) + [t + 2 for t in pre(b)[:6]]


def tiles_at(times, time):
    return [n for n, t in enumerate(times) if t == time]


class Batch:

    def __init__(self, pair, offset):
        self.pair, self.offset = pair, offset
        self.number = 2 * pair + offset
        self.parity = offset % 2

    def count(self, per_batch, done):
        return (2 * per_batch) * self.pair + (per_batch * self.offset + done)

    @property
    def first(self):
        return isinstance(self.number, int) and self.number == 0

    @property
    def second(self):
        return isinstance(self.number, int) and self.number == 1


def at_least(eng, sem, value):
    if not isinstance(value, int) or value > 0:
        eng.wait_ge(sem, value)


def two_layers(nc, x, adj, W, a, beta, weight, bias, out):
    B, N, C = x.shape
    T = N // P
    K = C // P
    HALF = N // 2
    TH = T // 2
    assert (T, K, W.shape[1], weight.shape[1]) == (8, 4, C, C)
    assert PARTS[-1] + 2 < GW[0] + 3
    assert max(GW_FIRST + ATT_FIRST) < 2 * SLOTS and max(PRE_FIRST + PRE) + 5 < 2 * SLOTS and PRE_SECOND[4:] == PRE[4:] and LEAD >= 0

    def live(pair, r):
        return {s: Batch(pair, r - s) for s in range(STAGES)}

    def run(eng, iteration, before_loop=None):
        def edge(r):
            batches = {s: b for s, b in live(0, r).items() if 0 <= b.offset < B}
            return {-1: Batch(0, 1), **batches} if r == 0 else batches
        for r in range(2):
            iteration(edge(r), edge(r - 1))
        if before_loop:
            before_loop()
        with eng.Fori(0, (B - 2) // 2) as pair:
            for r in (2, 3):
                iteration(live(pair, r), live(pair, r - 1))
        for r in (B, B + 1):
            iteration(edge(r), edge(r - 1))

    with ExitStack() as ctx:
        def sb(name, shape, dt):
            return ctx.enter_context(nc.sbuf_tensor(name, shape, dt))

        def sem(name):
            return ctx.enter_context(nc.semaphore(name))

        ident = sb("ident", [P, P], F32)
        minus_half = sb("minus_half", [P, 1], F32)
        betas = sb("betas", [P, 1], F32)
        peak = sb("peak", [P, 3], F32)
        peaks = sb("peaks", [P, 3], F32)
        bound = sb("bound", [P, 4], F32)
        pow2 = sb("pow2", [P, 4], F32)
        inv2 = sb("inv2", [P, 4], F32)
        scale = sb("scale", [P, 6], F32)
        w_scale, w2_scale, p_scale, g_scale, z_scale, o_factor = (scale[:, k:k + 1] for k in range(6))
        adj_sums = sb("adj_sums", [P, T], F32)
        adj_pow2 = sb("adj_pow2", [P, T], F32)
        adj_inv2 = sb("adj_inv2", [P, T], F32)
        adj_scales = sb("adj_scales", [P, T], F32)
        o_scales = sb("o_scales", [P, T], F32)
        low_sums = sb("low_sums", [P, T], F32)
        inexact = sb("inexact", [P, 1], I32)
        v_cols = sb("v_cols", [P, 2 * K], F32)
        v_rows = sb("v_rows", [P, 2, C], F32)
        bias_rows = sb("bias_rows", [P, C], F32)
        w_hi = sb("w_hi", [P, K, C], F16)
        w_lo = sb("w_lo", [P, K, C], F16)
        w2_hi = sb("w2_hi", [P, K, C], F16)
        w2_lo = sb("w2_lo", [P, K, C], F16)
        adjT_hi = sb("adjT_hi", [P, T, N], F16)
        adjT_lo = sb("adjT_lo", [P, T, N], F16)

        x_in = sb("x_in", [P, 4, C], F32)
        stats0 = sb("stats0", [P, T, 6], F32)
        mean0 = sb("mean0", [P, T, 2], F32)
        var0 = sb("var0", [P, T], F32)
        rstd0 = sb("rstd0", [P, T], F32)
        shift0 = sb("shift0", [P, T], F32)
        h0 = sb("h0", [P, 2, C], F32)
        h0_hi = sb("h0_hi", [P, 2, T, C], F16)
        h0_lo = sb("h0_lo", [P, 2, T, C], F16)
        junk = sb("junk", [P, C], F16)
        s1 = sb("s1", [P, 2, T], F32)
        s2 = sb("s2", [P, 2, T], F32)

        adj_in = sb("adj_in", [P, 2, N], F32)
        probs = sb("probs", [P, 2, N], F32)
        top = sb("top", [P, T], F32)
        minus_top = sb("minus_top", [P, T], F32)
        denom = sb("denom", [P, 2, T], F32)
        beta_denom = sb("beta_denom", [P, T], F32)
        inv_denom = sb("inv_denom", [P, T], F32)
        z_rows = sb("z_rows", [P, 2, T], F32)
        rows_hi = sb("rows_hi", [P, 2, N], F16)
        rows_lo = sb("rows_lo", [P, 2, N], F16)
        PT = sb("PT", [P, 2, T, N], F16)
        PT_hi, PT_lo = PT[:, 0], PT[:, 1]

        gT_hi = sb("gT_hi", [P, K, HALF], F16)
        gT_lo = sb("gT_lo", [P, K, HALF], F16)
        elu = sb("elu", [P, 2, C], F32)
        x1 = sb("x1", [P, T, C], F32)
        stats1 = sb("stats1", [P, T, 6], F32)
        mean1 = sb("mean1", [P, T, 2], F32)
        var1 = sb("var1", [P, T], F32)
        rstd1 = sb("rstd1", [P, T], F32)
        shift1 = sb("shift1", [P, T], F32)
        h1 = sb("h1", [P, 2, C], F32)
        h1_hi = sb("h1_hi", [P, T, C], F16)
        h1_lo = sb("h1_lo", [P, T, C], F16)

        yT_hi = sb("yT_hi", [P, K, N], F16)
        yT_lo = sb("yT_lo", [P, K, N], F16)

        W_in = x1[:, 0:K, :].rearrange("p k c -> p (k c)")
        w2_in = x1[:, K:2 * K, :].rearrange("p k c -> p (k c)")
        a_rows = h1
        abs_w = probs[:, :, :].rearrange("p u n -> p (u n)")
        adj_rows_hi, adj_rows_lo = (yT[:, :, :] for yT in (yT_hi, yT_lo))
        adj_stage = [tiles[:, 2 * k:2 * k + 4, :].rearrange("p t c -> p (t c)").bitcast(F32)
                     for tiles in (h1_hi, h1_lo) for k in (0, 2)]

        s2_rows = [ctx.enter_context(nc.psum_tensor(f"s2_rows{k}", [P, N], F32)) for k in range(2)]
        sums = [ctx.enter_context(nc.psum_tensor(f"sums{k}", [P, C], F32)) for k in range(4)]

        w_loaded = [sem(f"w_loaded{k}") for k in range(K)]
        w2_loaded = sem("w2_loaded")
        a_loaded = sem("a_loaded")
        bias_loaded = sem("bias_loaded")
        beta_loaded = sem("beta_loaded")
        consts_ready = sem("consts_ready")
        v_cols_ready = sem("v_cols_ready")
        v_spread = sem("v_spread")
        v_rows_ready = sem("v_rows_ready")
        w_summed = sem("w_summed")
        stage_loaded = [sem(f"stage_loaded{k}") for k in range(4)]
        adj_summed = sem("adj_summed")
        adj_scaled = sem("adj_scaled")
        peak_ready = sem("peak_ready")
        peaks_ready = sem("peaks_ready")
        scale_step = sem("scale_step")
        w_hi_ready = sem("w_hi_ready")
        w_split = sem("w_split")
        adj_hi_ready = sem("adj_hi_ready")
        adj_lo_ready = sem("adj_lo_ready")
        low_summed = sem("low_summed")
        adj_turned = [sem(f"adj_turned{k}") for k in range(4)]
        inexact_ready = sem("inexact_ready")

        x_loaded = [sem(f"x_loaded{k}") for k in range(4)]
        adj_loaded = [sem(f"adj_loaded{k}") for k in range(2)]
        x_reloaded = [sem(f"x_reloaded{k}") for k in range(T)]
        stored = [sem(f"stored{k}") for k in range(T)]
        stats0_taken = sem("stats0_taken")
        mean0_ready = sem("mean0_ready")
        var0_ready = sem("var0_ready")
        rstd0_ready = sem("rstd0_ready")
        shift0_ready = sem("shift0_ready")
        h0_ready = sem("h0_ready")
        h0_hi_ready = sem("h0_hi_ready")
        h0_lo_ready = sem("h0_lo_ready")
        s1_ready = sem("s1_ready")
        s2_ready = sem("s2_ready")
        s2_spread = sem("s2_spread")
        scores_ready = sem("scores_ready")
        leaky_ready = sem("leaky_ready")
        masked_ready = sem("masked_ready")
        minus_top_ready = sem("minus_top_ready")
        exp_ready = sem("exp_ready")
        beta_denom_ready = sem("beta_denom_ready")
        diag_added = sem("diag_added")
        inv_denom_ready = sem("inv_denom_ready")
        z_rows_ready = sem("z_rows_ready")
        rows_hi_ready = sem("rows_hi_ready")
        rows_lo_ready = sem("rows_lo_ready")
        rows_turned = [sem(f"rows_turned{k}") for k in range(2)]
        att_done = sem("att_done")
        gT_hi_ready = sem("gT_hi_ready")
        gT_lo_ready = sem("gT_lo_ready")
        gw_done = sem("gw_done")
        elu_exp_ready = sem("elu_exp_ready")
        elu_low_ready = sem("elu_low_ready")
        elu_ready = sem("elu_ready")
        x1_ready = sem("x1_ready")
        stats1_taken = sem("stats1_taken")
        mean1_ready = sem("mean1_ready")
        var1_ready = sem("var1_ready")
        rstd1_ready = sem("rstd1_ready")
        shift1_ready = sem("shift1_ready")
        h1_ready = sem("h1_ready")
        h1_hi_ready = sem("h1_hi_ready")
        h1_lo_ready = sem("h1_lo_ready")
        x1_bias_ready = sem("x1_bias_ready")
        y_done = sem("y_done")
        yT_hi_ready = sem("yT_hi_ready")
        yT_lo_ready = sem("yT_lo_ready")
        out_done = sem("out_done")
        result_ready = sem("result_ready")

        emptied = {"att": gT_lo_ready, "y": yT_lo_ready, "out": result_ready, "gw": elu_ready}

        def wait_apart(eng, *waits):
            waits = [(sem, value if isinstance(value, int) else eng.to_reg(value)) for sem, value in waits]
            eng.wait_ge(consts_ready, 3)
            for sem, value in waits:
                at_least(eng, sem, value)

        block = ctx.enter_context(nc.Block())

        @block.sync
        def _(sp):
            for k in range(2):
                sp.dma_start(a_rows[:, k, :], a[k * C:(k + 1) * C, 0].partition_broadcast(P)).then_inc(a_loaded, 16)
            for k in range(K):
                sp.dma_start(x1[:, k, :], W[k * P:(k + 1) * P, :]).then_inc(w_loaded[k], 16)
            sp.dma_start(betas[:, :], beta.partition_broadcast(P)).then_inc(beta_loaded, 16)

            def tile_of(tensor, b, n):
                return tensor[bass.ds(b.number, 1), n * P:(n + 1) * P, :].rearrange("o p c -> (o p) c")

            def step(b, time):
                for n in tiles_at(OUT, time):
                    sp.wait_ge(result_ready, b.count(T, n + 1))
                    sp.dma_start(tile_of(out, b, n), x1[:, n, :]).then_inc(stored[n], 16)
                for n in tiles_at(RELOAD_X_FIRST if b.first else RELOAD_X, time):
                    at_least(sp, stored[n], b.count(16, 0))
                    if b.first:
                        sp.wait_ge(w_split, 1 + n // K)
                    sp.dma_start(x1[:, n, :], tile_of(x, b, n)).then_inc(x_reloaded[n], 16)
                for n in tiles_at([t + 5 for t in pre(b)], time):
                    wait_apart(sp, (rows_lo_ready, b.count(T, n + 1)),
                                   (att_done, b.count(T, TH * (n // TH + 1) - T)))
                    for rows, turned in ((rows_hi, PT_hi), (rows_lo, PT_lo)):
                        sp.dma_start_transpose(turned[:, :, n * P:(n + 1) * P], rows[:, n % 2, :])\
                            .then_inc(rows_turned[n % 2], 16)
                for n in tiles_at(led(b, LOAD_X), time):
                    at_least(sp, h0_ready, b.count(T, n + 1 - 4))
                    sp.dma_start(x_in[:, n % 4, :], tile_of(x, b, n)).then_inc(x_loaded[n % 4], 16)
                for n in tiles_at(load_adj(b), time):
                    at_least(sp, masked_ready, b.count(T, n + 1 - 2))
                    sp.dma_start(adj_in[:, n % 2, :], adj[n * P:(n + 1) * P, :]).then_inc(adj_loaded[n % 2], 16)

            def setup(time):
                if time == LOAD_W2:
                    sp.dma_start(w2_in.rearrange("p (k c) -> p k c", k=K), weight.rearrange("(k p) c -> p k c", p=P))\
                        .then_inc(w2_loaded, 16)
                    sp.dma_start(bias_rows[:, :], bias.partition_broadcast(P)).then_inc(bias_loaded, 16)
                for n in tiles_at(LOAD_STAGE, time):
                    if n >= 4:
                        sp.wait_ge(low_summed, n + 1 - 4)
                    sp.dma_start(adj_stage[n % 4], adj[n * P:(n + 1) * P, :]).then_inc(stage_loaded[n % 4], 16)
                for n in tiles_at([t + 1 for t in PARTS], time):
                    sp.wait_ge(adj_lo_ready, n + 1)
                    for rows, turned in ((adj_rows_hi, adjT_hi), (adj_rows_lo, adjT_lo)):
                        sp.dma_start_transpose(turned[:, :, n * P:(n + 1) * P], rows[:, n % 4, :])\
                            .then_inc(adj_turned[n % 4], 16)

            def iteration(batches, _):
                for slot in range(SLOTS):
                    for stage in sorted(batches, reverse=True):
                        step(batches[stage], SLOTS * stage + slot)
                        if batches[stage].first:
                            setup(SLOTS * stage + slot)

            run(sp, iteration)
            for n in range(T):
                sp.wait_ge(stored[n], 16 * B)

        @block.gpsimd
        def _(pool):
            pool.memset(ident[:, :], 0.0).then_inc(consts_ready, 1)
            pool.memset(minus_half[:, :], -0.5).then_inc(consts_ready, 1)
            pool.wait_ge(consts_ready, 1)
            pool.affine_select(out=ident[:, :], in_=ident[:, :], compare_op=ALU.not_equal, fill=1.0, base=0,
                               pattern=[[-1, P]], channel_multiplier=1).then_inc(consts_ready, 1)
            pool.wait_ge(consts_ready, 3)
            pool.wait_ge(beta_loaded, 16)

            def norm_scale(b, n, mean_sem, mean, var_sem, var, rstd_sem, rstd, shift_sem, shift):
                wait_apart(pool, (mean_sem, b.count(T, n + 1)))
                pool.tensor_scalar(var[:, n:n + 1], mean[:, n, 1:2], H_SCALE ** -2, EPS * H_SCALE ** -2,
                                   ALU.mult, ALU.add).then_inc(var_sem, 1)
                pool.wait_ge(var_sem, b.count(T, n + 1))
                pool.tensor_tensor(rstd[:, n:n + 1], var[:, n:n + 1], minus_half[:, :], ALU.pow).then_inc(rstd_sem, 1)
                wait_apart(pool, (rstd_sem, b.count(T, n + 1)))
                pool.tensor_scalar(shift[:, n:n + 1], mean[:, n, 0:1], rstd[:, n:n + 1], -1.0,
                                   ALU.mult, ALU.mult).then_inc(shift_sem, 1)

            def step(b, time):
                for n in tiles_at([t + 1 for t in GW], time):
                    norm_scale(b, n, mean1_ready, mean1, var1_ready, var1, rstd1_ready, rstd1, shift1_ready, shift1)
                for n in tiles_at([t + 1 for t in pre(b)], time):
                    wait_apart(pool, (masked_ready, b.count(T, n + 1)))
                    pool.tensor_scalar(minus_top[:, n:n + 1], top[:, n:n + 1], -1.0, None, ALU.mult)\
                        .then_inc(minus_top_ready, 1)
                for n in tiles_at([t + 2 for t in pre(b)], time):
                    wait_apart(pool, (exp_ready, b.count(T, n + 1)),
                                     (diag_added, b.count(T, n + 1 - T)))
                    pool.tensor_scalar(beta_denom[:, n:n + 1], denom[:, b.parity, n:n + 1], betas[:, 0:1], None, ALU.mult)\
                        .then_inc(beta_denom_ready, 1)
                for n in tiles_at(led(b, NORM0), time):
                    norm_scale(b, n, mean0_ready, mean0, var0_ready, var0, rstd0_ready, rstd0, shift0_ready, shift0)
                for n in tiles_at([t + 3 for t in GW], time):
                    pool.wait_ge(h1_hi_ready, b.count(T, n + 1))
                    pool.tensor_tensor(h1_lo[:, n, :], h1[:, n % 2, :], h1_hi[:, n, :], ALU.subtract)\
                        .then_inc(h1_lo_ready, 1)
                for n in tiles_at([t + 8 for t in GW], time):
                    pool.tensor_tensor(x1[:, n, :], x1[:, n, :], bias_rows[:, :], ALU.add).then_inc(x1_bias_ready, 1)
                for n in tiles_at([t + 1 for t in led(b, H0)], time):
                    pool.wait_ge(h0_hi_ready, b.count(T, n + 1))
                    at_least(pool, att_done, b.count(T, -T))
                    pool.tensor_tensor(h0_lo[:, b.parity, n, :], h0[:, n % 2, :], h0_hi[:, b.parity, n, :], ALU.subtract)\
                        .then_inc(h0_lo_ready, 1)

            def group(b, time):
                for n in tiles_at(gw(b), time):
                    pool.wait_ge(elu_ready, b.count(T, n + 1))
                    pool.wait_ge(x_reloaded[n], b.count(16, 16))
                    pool.tensor_tensor(x1[:, n, :], x1[:, n, :], elu[:, n % 2, :], ALU.add).then_inc(x1_ready, 1)

            def setup(time):
                if time == SCALES - 1:
                    pool.wait_ge(w_summed, 2)
                    pool.partition_all_reduce(peaks[:, 0:2], peak[:, 0:2], P, ABSMAX).then_inc(peaks_ready, 1)
                    pool.wait_ge(bias_loaded, 16)
                if time == INEXACT:
                    pool.wait_ge(peak_ready, 1)
                    pool.partition_all_reduce(peaks[:, 2:3], peak[:, 2:3], P, ABSMAX).then_inc(peaks_ready, 1)

            def iteration(batches, _):
                for slot in range(SLOTS):
                    for stage in sorted(batches, reverse=True):
                        step(batches[stage], SLOTS * stage + slot)
                        if batches[stage].first:
                            setup(SLOTS * stage + slot)
                    for stage in batches:
                        group(batches[stage], SLOTS * stage + slot)

            run(pool, iteration)

        @block.scalar
        def _(act):
            def setup(time):
                for k in tiles_at(SUM_W, time):
                    for loaded in (w_loaded, [w2_loaded])[k]:
                        act.wait_ge(loaded, 16)
                    if k == 1:
                        act.wait_ge(w_summed, 1)
                    act.activation(abs_w, (W_in, w2_in)[k], ACT.Abs, accum_out=peak[:, k:k + 1]).then_inc(w_summed, 1)
                if time == H0[0]:
                    act.wait_ge(v_spread, 1)
                    act.activation(v_rows[:, :, :].rearrange("p k c -> p (k c)"), s2_rows[0][:, :], ACT.Copy).then_inc(v_rows_ready, 1)
                if time == SCALES + 1:
                    act.wait_ge(scale_step, SCALE_STEPS)
                for k in tiles_at(SPLIT, time):
                    act.activation((w_hi, w2_hi)[k][:, :, :].rearrange("p k c -> p (k c)"), (W_in, w2_in)[k], ACT.Copy,
                                   scale=(w_scale, w2_scale)[k]).then_inc(w_hi_ready, 1)
                for n in tiles_at(SUM_ADJ, time):
                    act.wait_ge(stage_loaded[n % 4], 16 * (n // 4 + 1))
                    if n >= 4:
                        act.wait_ge(adj_turned[n % 4], 32)
                    act.activation(adj_rows_hi[:, n % 4, :], adj_stage[n % 4], ACT.Abs, accum_out=adj_sums[:, n:n + 1])\
                        .then_inc(adj_summed, 1)
                for n in tiles_at(PARTS, time):
                    act.wait_ge(adj_scaled, 5 * (n // 4 + 1))
                    act.activation(adj_rows_hi[:, n % 4, :], adj_stage[n % 4], ACT.Copy, scale=adj_scales[:, n:n + 1])\
                        .then_inc(adj_hi_ready, 1)
                for n in tiles_at([t + 2 for t in PARTS], time):
                    act.wait_ge(adj_lo_ready, n + 1)
                    act.activation(adj_stage[n % 4].bitcast(F16)[:, 0:N], adj_rows_lo[:, n % 4, :], ACT.Abs,
                                   accum_out=low_sums[:, n:n + 1]).then_inc(low_summed, 1)

            def step(b, time):
                for n in tiles_at([t + 4 for t in pre(b)], time):
                    act.wait_ge(diag_added, b.count(T, n + 1))
                    at_least(act, rows_turned[n % 2], b.count(128, 32 * (n // 2)))
                    act.activation(rows_hi[:, n % 2, :], probs[:, n % 2, :], ACT.Copy, scale=p_scale)\
                        .then_inc(rows_hi_ready, 1)
                for n in tiles_at([t + 2 for t in pre(b)], time):
                    act.wait_ge(minus_top_ready, b.count(T, n + 1))
                    act.activation(probs[:, n % 2, :], probs[:, n % 2, :], ACT.Exp, bias=minus_top[:, n:n + 1],
                                   accum_out=denom[:, b.parity, n:n + 1]).then_inc(exp_ready, 1)
                for n in tiles_at([t + 3 for t in GW], time):
                    act.wait_ge(h1_ready, b.count(T, n + 1))
                    act.activation(h1_hi[:, n, :], h1[:, n % 2, :], ACT.Copy).then_inc(h1_hi_ready, 1)
                for n in tiles_at([t + 2 for t in GW], time):
                    act.wait_ge(shift1_ready, b.count(T, n + 1))
                    at_least(act, h1_lo_ready, b.count(T, n + 1 - 2))
                    act.activation(h1[:, n % 2, :], x1[:, n, :], ACT.Relu, bias=shift1[:, n:n + 1],
                                   scale=rstd1[:, n:n + 1]).then_inc(h1_ready, 1)
                for n in tiles_at([t + 1 for t in led(b, H0)], time):
                    act.wait_ge(h0_ready, b.count(T, n + 1))
                    at_least(act, att_done, b.count(T, -T))
                    act.activation(h0_hi[:, b.parity, n, :], h0[:, n % 2, :], ACT.Copy).then_inc(h0_hi_ready, 1)
                for n in tiles_at(led(b, H0), time):
                    act.wait_ge(shift0_ready, b.count(T, n + 1))
                    at_least(act, h0_lo_ready, b.count(T, n + 1 - 2))
                    at_least(act, s2_ready, b.count(T, n + 1 - 2))
                    act.activation(h0[:, n % 2, :], x_in[:, n % 4, :], ACT.Relu, bias=shift0[:, n:n + 1],
                                   scale=rstd0[:, n:n + 1]).then_inc(h0_ready, 1)
                for n in tiles_at(pre(b), time):
                    act.wait_ge(s2_spread, b.count(T, T))
                    at_least(act, rows_lo_ready, b.count(T, n + 1 - 2))
                    if b.first and n == 0:
                        act.wait_ge(w_summed, 2)
                    act.activation(probs[:, n % 2, :], s2_rows[b.parity][:, :], ACT.Identity, bias=s1[:, b.parity, n:n + 1])\
                        .then_inc(scores_ready, 1)

            def group(b, time):
                for n in tiles_at(att(b), time):
                    half, c = divmod(n, K)
                    act.wait_ge(att_done, b.count(T, n + 1))
                    act.activation(gT_hi[:, c, :], sums[c][:, :], ACT.Copy, scale=g_scale).then_inc(gT_hi_ready, 1)
                for n in tiles_at(gw(b), time):
                    act.wait_ge(gw_done, b.count(T, n + 1))
                    act.wait_ge(z_rows_ready, b.count(1, 1))
                    at_least(act, x1_ready, b.count(T, n + 1 - 2))
                    act.activation(elu[:, n % 2, :], sums[n % 4][:, :], ACT.Exp, scale=z_rows[:, b.parity, n:n + 1])\
                        .then_inc(elu_exp_ready, 1)
                for n in tiles_at(Y, time):
                    half, d = divmod(n, K)
                    act.wait_ge(y_done, b.count(T, n + 1))
                    act.activation(yT_hi[:, d, half * HALF:(half + 1) * HALF], sums[d][:, :], ACT.Copy,
                                   scale=Y_SCALE / (TOP * H_SCALE)).then_inc(yT_hi_ready, 1)

            def iteration(batches, _):
                for slot in range(SLOTS):
                    for stage in sorted(batches, reverse=True):
                        step(batches[stage], SLOTS * stage + slot)
                        if batches[stage].first:
                            setup(SLOTS * stage + slot)
                    for stage in batches:
                        group(batches[stage], SLOTS * stage + slot)

            run(act, iteration)

        @block.vector
        def _(dve):
            dve.wait_ge(a_loaded, 32)
            for k in range(2 * K):
                dve.wait_ge(w_loaded[k % K], 16)
                if k >= 1:
                    dve.wait_ge(v_cols_ready, k)
                dve.tensor_tensor_reduce(junk[:, :], W_in[:, (k % K) * C:(k % K + 1) * C], a_rows[:, k // K, :],
                                         1.0 / H_SCALE, 0.0, ALU.mult, ALU.add, v_cols[:, k:k + 1]).then_inc(v_cols_ready, 1)

            def power_below(pow2, inv2, bound, sem_done, count):
                dve.tensor_scalar(pow2.bitcast(I32), bound.bitcast(I32), EXPONENT, None, ALU.bitwise_and).then_inc(sem_done, 1)
                dve.wait_ge(sem_done, count + 1)
                dve.reciprocal(inv2, pow2).then_inc(sem_done, 1)
                dve.wait_ge(sem_done, count + 2)

            def scales():
                dve.wait_ge(beta_loaded, 16)
                dve.scalar_tensor_tensor(bound[:, 3:4], betas[:, :], -1.0, betas[:, :], ALU.mult, ALU.max).then_inc(scale_step, 1)
                dve.wait_ge(scale_step, 1)
                dve.tensor_scalar(bound[:, 2:3], bound[:, 3:4], float(N), 1.0, ALU.mult, ALU.add).then_inc(scale_step, 1)
                dve.wait_ge(scale_step, 2)
                dve.tensor_scalar(bound[:, 3:4], bound[:, 3:4], 1.0, None, ALU.add).then_inc(scale_step, 1)
                dve.wait_ge(peaks_ready, 1)
                dve.tensor_scalar(bound[:, 0:2], peaks[:, 0:2], TINY, None, ALU.max).then_inc(scale_step, 1)
                dve.wait_ge(scale_step, 4)
                power_below(pow2[:, :], inv2[:, :], bound[:, :], scale_step, 4)
                dve.tensor_scalar(scale[:, 0:3], inv2[:, 0:3], TOP, None, ALU.mult).then_inc(scale_step, 1)
                dve.tensor_scalar(bound[:, 0:1], pow2[:, 2:3], 1.0 / (H_SCALE * TOP), None, ALU.mult).then_inc(scale_step, 1)
                dve.tensor_scalar(bound[:, 1:2], pow2[:, 3:4], 1.0 / TOP, None, ALU.mult).then_inc(scale_step, 1)
                dve.tensor_scalar(o_factor, pow2[:, 1:2], 1.0 / (TOP * Y_SCALE), None, ALU.mult).then_inc(scale_step, 1)
                dve.wait_ge(scale_step, 9)
                dve.tensor_tensor(g_scale, bound[:, 0:1], inv2[:, 3:4], ALU.mult).then_inc(scale_step, 1)
                dve.tensor_tensor(z_scale, bound[:, 1:2], pow2[:, 0:1], ALU.mult).then_inc(scale_step, 1)
                dve.wait_ge(scale_step, SCALE_STEPS)

            def setup(time):
                if time == H0[0]:
                    dve.wait_ge(v_rows_ready, 1)
                if time == SCALES:
                    scales()
                for k in tiles_at(SPLIT, time):
                    hi, lo = ((w_hi, w_lo), (w2_hi, w2_lo))[k]
                    dve.wait_ge(w_hi_ready, k + 1)
                    dve.scalar_tensor_tensor(lo[:, :, :].rearrange("p k c -> p (k c)"), (W_in, w2_in)[k], (w_scale, w2_scale)[k],
                                             hi[:, :, :].rearrange("p k c -> p (k c)"), ALU.mult, ALU.subtract).then_inc(w_split, 1)
                for group in tiles_at(SCALE_ADJ, time):
                    tiles, before = slice(4 * group, 4 * group + 4), 5 * group
                    dve.wait_ge(adj_summed, 4 * group + 4)
                    dve.tensor_scalar(adj_sums[:, tiles], adj_sums[:, tiles], TINY, None, ALU.max).then_inc(adj_scaled, 1)
                    dve.wait_ge(adj_scaled, before + 1)
                    power_below(adj_pow2[:, tiles], adj_inv2[:, tiles], adj_sums[:, tiles], adj_scaled, before + 1)
                    dve.tensor_scalar(adj_scales[:, tiles], adj_inv2[:, tiles], TOP, None, ALU.mult).then_inc(adj_scaled, 1)
                    dve.tensor_scalar(o_scales[:, tiles], adj_pow2[:, tiles], o_factor, None, ALU.mult).then_inc(adj_scaled, 1)
                    dve.wait_ge(adj_scaled, before + 5)
                for n in tiles_at(PARTS, time):
                    dve.wait_ge(adj_hi_ready, n + 1)
                    if n >= 4:
                        dve.wait_ge(low_summed, n + 1 - 4)
                    dve.scalar_tensor_tensor(adj_rows_lo[:, n % 4, :], adj_stage[n % 4], adj_scales[:, n:n + 1], adj_rows_hi[:, n % 4, :],
                                             ALU.mult, ALU.subtract).then_inc(adj_lo_ready, 1)
                if time == INEXACT:
                    dve.wait_ge(low_summed, T)
                    dve.tensor_reduce(peak[:, 2:3], low_sums[:, :], AX.X, ALU.max).then_inc(peak_ready, 1)
                    dve.wait_ge(peaks_ready, 2)
                    dve.tensor_scalar(inexact[:, :], peaks[:, 2:3], 0.0, None, ALU.is_gt).then_inc(inexact_ready, 1)

            def step(b, time):
                for n in tiles_at([t + 4 for t in pre(b)], time):
                    dve.wait_ge(rows_hi_ready, b.count(T, n + 1))
                    dve.scalar_tensor_tensor(rows_lo[:, n % 2, :], probs[:, n % 2, :], p_scale, rows_hi[:, n % 2, :],
                                             ALU.mult, ALU.subtract).then_inc(rows_lo_ready, 1)
                for n in tiles_at([t + 3 for t in pre(b)], time):
                    own = probs[:, n % 2, n * P:(n + 1) * P]
                    dve.wait_ge(beta_denom_ready, b.count(T, n + 1))
                    dve.scalar_tensor_tensor(own, ident[:, :], beta_denom[:, n:n + 1], own, ALU.mult, ALU.add)\
                        .then_inc(diag_added, 1)
                if time == (RECIP_FIRST if b.first else RECIP):
                    dve.wait_ge(exp_ready, b.count(T, T))
                    at_least(dve, z_rows_ready, b.count(1, 0))
                    dve.reciprocal(inv_denom[:, :], denom[:, b.parity, :]).then_inc(inv_denom_ready, 1)
                    dve.wait_ge(inv_denom_ready, b.count(1, 1))
                    dve.tensor_scalar(z_rows[:, b.parity, :], inv_denom[:, :], z_scale, None, ALU.mult).then_inc(z_rows_ready, 1)
                for n in tiles_at([t + 1 for t in GW], time):
                    dve.wait_ge(x1_ready, b.count(T, n + 1))
                    dve.bn_stats(stats1[:, n, :], x1[:, n, :]).then_inc(stats1_taken, 1)
                    wait_apart(dve, (stats1_taken, b.count(T, n + 1)))
                    dve.bn_aggr(mean1[:, n, :], stats1[:, n, :]).then_inc(mean1_ready, 1)
                for n in tiles_at([t + 1 for t in pre(b)], time):
                    own = probs[:, n % 2, :]
                    dve.wait_ge(scores_ready, b.count(T, n + 1))
                    dve.scalar_tensor_tensor(own, own, SLOPE, own, ALU.mult, ALU.max).then_inc(leaky_ready, 1)
                    wait_apart(dve, (leaky_ready, b.count(T, n + 1)),
                                    (adj_loaded[n % 2], b.count(64, 16 * (n // 2 + 1))))
                    dve.tensor_tensor_reduce(own, own, adj_in[:, n % 2, :], 1.0, -HUGE, ALU.mult, ALU.max, top[:, n:n + 1])\
                        .then_inc(masked_ready, 1)
                for n in tiles_at([t + 1 for t in led(b, H0)], time):
                    dve.wait_ge(h0_ready, b.count(T, n + 1))
                    at_least(dve, s2_ready, b.count(T, n))
                    dve.tensor_tensor_reduce(junk[:, :], h0[:, n % 2, :], v_rows[:, 0, :], 1.0, 0.0, ALU.mult, ALU.add,
                                             s1[:, b.parity, n:n + 1]).then_inc(s1_ready, 1)
                    dve.wait_ge(s1_ready, b.count(T, n + 1))
                    dve.tensor_tensor_reduce(junk[:, :], h0[:, n % 2, :], v_rows[:, 1, :], 1.0, 0.0, ALU.mult, ALU.add,
                                             s2[:, b.parity, n:n + 1]).then_inc(s2_ready, 1)
                for n in tiles_at(led(b, NORM0), time):
                    dve.wait_ge(x_loaded[n % 4], b.count(32, 16 * (n // 4 + 1)))
                    dve.bn_stats(stats0[:, n, :], x_in[:, n % 4, :]).then_inc(stats0_taken, 1)
                    wait_apart(dve, (stats0_taken, b.count(T, n + 1)))
                    dve.bn_aggr(mean0[:, n, :], stats0[:, n, :]).then_inc(mean0_ready, 1)

            def group(b, time):
                for n in tiles_at(att(b), time):
                    c = n % K
                    dve.wait_ge(gT_hi_ready, b.count(T, n + 1))
                    dve.scalar_tensor_tensor(gT_lo[:, c, :], sums[c][:, :], g_scale, gT_hi[:, c, :], ALU.mult, ALU.subtract)\
                        .then_inc(gT_lo_ready, 1)
                for n in tiles_at(gw(b), time):
                    own = elu[:, n % 2, :]
                    dve.wait_ge(elu_exp_ready, b.count(T, n + 1))
                    dve.tensor_scalar(own, own, 1.0, -1.0, ALU.min, ALU.add).then_inc(elu_low_ready, 1)
                    dve.wait_ge(elu_low_ready, b.count(T, n + 1))
                    dve.scalar_tensor_tensor(own, sums[n % 4][:, :], z_rows[:, b.parity, n:n + 1], own, ALU.mult, ALU.max)\
                        .then_inc(elu_ready, 1)
                for n in tiles_at(Y, time):
                    half, d = divmod(n, K)
                    dve.wait_ge(yT_hi_ready, b.count(T, n + 1))
                    dve.scalar_tensor_tensor(yT_lo[:, d, half * HALF:(half + 1) * HALF], sums[d][:, :], Y_SCALE / (TOP * H_SCALE),
                                             yT_hi[:, d, half * HALF:(half + 1) * HALF], ALU.mult, ALU.subtract)\
                        .then_inc(yT_lo_ready, 1)
                for n in tiles_at(OUT, time):
                    dve.wait_ge(out_done, b.count(T, n + 1))
                    dve.wait_ge(x1_bias_ready, b.count(T, n + 1))
                    dve.scalar_tensor_tensor(x1[:, n, :], sums[n % 4][:, :], o_scales[:, n:n + 1], x1[:, n, :], ALU.mult, ALU.add)\
                        .then_inc(result_ready, 1)

            def iteration(batches, _):
                for slot in range(SLOTS):
                    for stage in sorted(batches, reverse=True):
                        step(batches[stage], SLOTS * stage + slot)
                        if batches[stage].first:
                            setup(SLOTS * stage + slot)
                    for stage in batches:
                        group(batches[stage], SLOTS * stage + slot)

            run(dve, iteration)

        @block.tensor
        def _(pe):
            def spread(into, k, column):
                return pe.transpose(into[:, k * P:(k + 1) * P], column.to_broadcast([P, P]), ident[:, :])

            pe.wait_ge(consts_ready, 3)
            for k in range(2 * K):
                pe.wait_ge(v_cols_ready, k + 1)
                last = spread(s2_rows[0], k, v_cols[:, k:k + 1])
            last.then_inc(v_spread, 1)
            low = []

            def before_loop():
                pe.wait_ge(w_split, 2)
                for turned in adj_turned:
                    pe.wait_ge(turned, 64)
                pe.wait_ge(inexact_ready, 1)
                low.append(pe.value_load(inexact[0:1, 0:1], min_val=0, max_val=1))

            def bank_free(k, i, batches, last_batches):
                for back in range(1, len(BLOCKS)):
                    kind, half, stage = BLOCKS[k - back]
                    present = batches if back <= k else last_batches
                    if stage in present:
                        at_least(pe, emptied[kind], present[stage].count(T, TH * half + i + 1))
                        return

            def products(bank, pairs):
                for j, (stationary, moving) in enumerate(pairs):
                    last = pe.matmul(bank, stationary, moving, start=(j == 0), stop=(j == len(pairs) - 1))
                return last

            def y_terms(d, half, tiles, start=False, stop=False):
                cols, rows = slice(d * P, (d + 1) * P), slice(half * HALF, (half + 1) * HALF)
                for j in tiles:
                    pe.matmul(sums[d][:, :], h1_hi[:, j, cols], adjT_hi[:, j, rows], start=(start and j == tiles[0]), stop=False)
                if stop:
                    with pe.If(low[0] > 0):
                        for j in range(T):
                            pe.matmul(sums[d][:, :], h1_hi[:, j, cols], adjT_lo[:, j, rows], start=False, stop=False)
                for j in tiles:
                    last = pe.matmul(sums[d][:, :], h1_lo[:, j, cols], adjT_hi[:, j, rows], start=False,
                                     stop=(stop and j == tiles[-1]))
                return last

            def group(b, time, batches, last_batches):
                if b.first and time in ATT_FIRST + GW_FIRST:
                    if time in GW_FIRST:
                        pe.wait_ge(gT_lo_ready, GW_FIRST.index(time) + 1)
                    elif time in ATT_FIRST[TH:]:
                        pe.wait_ge(elu_ready, ATT_FIRST.index(time) + 1 - TH)
                else:
                    bank_free((time % SLOTS) // TH, time % TH, batches, last_batches)
                for n in tiles_at(att(b), time):
                    half, c = divmod(n, K)
                    cols, rows = slice(c * P, (c + 1) * P), slice(half * HALF, (half + 1) * HALF)
                    if c == 0:
                        for turned in rows_turned:
                            pe.wait_ge(turned, b.count(128, 64 * (half + 1)))
                        pe.wait_ge(h0_lo_ready, b.count(T, T))
                    products(sums[c][:, :], [
                        pair for j in range(T) for pair in (
                            (h0_hi[:, b.parity, j, cols], PT_hi[:, j, rows]),
                            (h0_hi[:, b.parity, j, cols], PT_lo[:, j, rows]),
                            (h0_lo[:, b.parity, j, cols], PT_hi[:, j, rows]))
                    ]).then_inc(att_done, 1)
                for n in tiles_at(gw(b), time):
                    rows = slice((n % TH) * P, (n % TH + 1) * P)
                    if b.first and n == 0:
                        pe.wait_ge(w_split, 1)
                    pe.wait_ge(gT_lo_ready, b.count(T, TH * (n // TH + 1)))
                    products(sums[n % 4][:, :], [
                        pair for c in range(K) for pair in (
                            (gT_hi[:, c, rows], w_hi[:, c, :]),
                            (gT_hi[:, c, rows], w_lo[:, c, :]),
                            (gT_lo[:, c, rows], w_hi[:, c, :]))
                    ]).then_inc(gw_done, 1)
                for n in tiles_at(Y, time):
                    half, d = divmod(n, K)
                    early = len(batches) == 1 and half == 0
                    if early and n == 0:
                        pe.wait_ge(h1_lo_ready, b.count(T, TH))
                        for d_early in range(K):
                            bank_free((time % SLOTS) // TH, d_early, batches, last_batches)
                            y_terms(d_early, half, range(TH), start=True)
                    if n == 0:
                        pe.wait_ge(h1_lo_ready, b.count(T, T))
                    y_terms(d, half, range(TH, T) if early else range(T), start=not early, stop=True).then_inc(y_done, 1)
                for n in tiles_at(OUT, time):
                    rows = slice(n * P, (n + 1) * P)
                    pe.wait_ge(yT_lo_ready, b.count(T, TH * (n // TH + 1)))
                    products(sums[n % 4][:, :], [
                        pair for d in range(K) for pair in (
                            (yT_hi[:, d, rows], w2_hi[:, d, :]),
                            (yT_hi[:, d, rows], w2_lo[:, d, :]),
                            (yT_lo[:, d, rows], w2_hi[:, d, :]))
                    ]).then_inc(out_done, 1)

            def step(b, time):
                for n in tiles_at(led(b, SPREAD), time):
                    pe.wait_ge(s2_ready, b.count(T, n + 1))
                    if n == 0:
                        at_least(pe, scores_ready, b.count(T, -T))
                        if b.first:
                            pe.wait_ge(v_rows_ready, 1)
                    spread(s2_rows[b.parity], n, s2[:, b.parity, n:n + 1]).then_inc(s2_spread, 1)

            def iteration(batches, last_batches):
                for slot in range(SLOTS):
                    for stage in batches:
                        time = SLOTS * stage + slot
                        if time in att(batches[stage]) + gw(batches[stage]) + Y + OUT:
                            group(batches[stage], time, batches, last_batches)
                    for stage in sorted(batches, reverse=True):
                        step(batches[stage], SLOTS * stage + slot)

            run(pe, iteration, before_loop)


_INS = ["x", "adj", "L0_gnn_W", "L0_gnn_a", "L0_gnn_beta", "L1_gnn_weight", "L1_gnn_bias"]
_OUTS = [((16, 1024, 512), "float32")]


def kernel(**inputs):
    import numpy as _np
    import concourse.bacc as _bacc
    from concourse import mybir as _mybir
    from concourse.bass_utils import run_bass_kernel_spmd as _run

    nc = _bacc.Bacc("TRN2", target_bir_lowering=False, num_devices=1, dynamic_dma_scratch_size=1024)
    arrays, args = {}, []
    for name in _INS:
        a = _np.ascontiguousarray(inputs[name])
        arrays[f"in_{name}_dram"] = a
        args.append(nc.dram_tensor(f"in_{name}_dram", a.shape, _mybir.dt.from_np(a.dtype), kind="ExternalInput").ap())
    for i, (shape, dtype) in enumerate(_OUTS):
        dt = _mybir.dt.from_np(_np.dtype(dtype))
        args.append(nc.dram_tensor(f"out_{i}_dram", shape, dt, kind="ExternalOutput").ap())
    two_layers(nc, *args)
    r = _run(nc, [arrays], core_ids=[0])
    return r.results[0]["out_0_dram"]
```
